# Optimizing a Trainium2 kernel written in Bass

```python
import numpy as np
import jax
import jax.numpy as jnp

def _softmax(x, axis=-1):
    return jax.nn.softmax(x, axis=axis)

def _gelu(x):
    return jax.nn.gelu(x, approximate=True)

def _silu(x):
    return jax.nn.silu(x)

def _sigmoid(x):
    return jax.nn.sigmoid(x)

def _layernorm(x, axis=-1, eps=1e-05):
    m = jnp.mean(x, axis=axis, keepdims=True)
    v = jnp.var(x, axis=axis, keepdims=True)
    return (x - m) / jnp.sqrt(v + eps)

def _scatter_add(tgt, idx, src, axis=0):
    return tgt.at[idx].add(src)

def _segment_sum(src, seg, n):
    return jax.ops.segment_sum(src, seg, n)
kernel_name = 'mk_cond_seq_d4_seqx_r8_6e42ae'

def setup_inputs(seed: int=0):
    np.random.seed(seed)
    _w = jnp.asarray

    def _rec_inputs():
        import jax
        import jax.numpy as jnp
        _rk = jax.random.key(seed)
        x = -1.528e-05 + 0.9999 * jax.random.normal(jax.random.fold_in(_rk, 1), (32, 32, 256), jnp.float32)
        _lenS = 32 - jax.random.randint(jax.random.fold_in(_rk, 7), (32,), 0, max(1, 32 // 4) + 1, jnp.int32)
        _lenS2 = 32 - jax.random.randint(jax.random.fold_in(_rk, 8), (32,), 0, max(1, 32 // 4) + 1, jnp.int32)
        itok_B_1_2 = jax.random.randint(jax.random.fold_in(_rk, 11), (32,), 1, 3, jnp.int32)
        itok_B_17_1546 = jax.random.randint(jax.random.fold_in(_rk, 13), (32,), 17, 1547, jnp.int32)
        return (x, itok_B_1_2, itok_B_17_1546, _lenS)
    x, itok_B_1_2, itok_B_17_1546, _lenS = _rec_inputs()

    def _L0_cond_setup():
        import jax, jax.numpy as jnp
        import numpy as np
        H = 256
        K = 128
        R = 3
        B = 8
        S = 256
        LN_EPS = 1e-05
        key = jax.random.key(seed)
        ks = jax.random.split(key, 8)
        sd_d = 1.0 / np.sqrt(H)
        sd_u = 1.0 / np.sqrt(K)
        return {'role': jax.random.randint(ks[0], (B,), 0, R), 'hidden_states': jax.random.normal(ks[1], (B, S, H), dtype=jnp.float32), 'W_down': jax.random.uniform(ks[2], (R, H, K), jnp.float32, -sd_d, sd_d), 'b_down': jax.random.uniform(ks[3], (R, K), jnp.float32, -sd_d, sd_d), 'W_up': jax.random.uniform(ks[4], (R, K, H), jnp.float32, -sd_u, sd_u), 'b_up': jax.random.uniform(ks[5], (R, H), jnp.float32, -sd_u, sd_u), 'gamma': jnp.ones((R, H), jnp.float32), 'beta': jnp.zeros((R, H), jnp.float32)}
    _L0_cond_all = _L0_cond_setup()
    _L0_cond_in = {k: v for k, v in _L0_cond_all.items() if k in ('W_down', 'b_down', 'W_up', 'b_up', 'gamma', 'beta')}
    del _L0_cond_all

    def _L1_cond_setup():
        import jax, jax.numpy as jnp
        import numpy as np
        B, T, V = (8, 64, 256)
        H = 4 * V
        key = jax.random.key(seed)
        ks = jax.random.split(key, 16)
        s = lambda n: 1.0 / np.sqrt(n)
        inp = {'x': jax.random.uniform(ks[0], (B, T, V), dtype=jnp.float32), 'lens': jax.random.randint(ks[1], (B,), 1, T, dtype=jnp.int64), 'target_codes': jax.random.randint(ks[2], (B,), 0, V, dtype=jnp.int64), 'Wq': jax.random.normal(ks[3], (V, V), jnp.float32) * s(V), 'Wk': jax.random.normal(ks[4], (V, V), jnp.float32) * s(V), 'Wv': jax.random.normal(ks[5], (V, V), jnp.float32) * s(V), 'Wp': jax.random.normal(ks[6], (V, V), jnp.float32) * s(V), 'bp': jnp.zeros((V,), jnp.float32), 'cW1': jax.random.normal(ks[7], (V, H), jnp.float32) * s(V), 'cb1': jnp.zeros((H,), jnp.float32), 'cW2': jax.random.normal(ks[8], (H, V), jnp.float32) * s(H), 'cb2': jnp.zeros((V,), jnp.float32), 'mW1': jax.random.normal(ks[9], (2 * V, H), jnp.float32) * s(2 * V), 'mb1': jnp.zeros((H,), jnp.float32), 'mW2': jax.random.normal(ks[10], (H, V), jnp.float32) * s(H), 'mb2': jnp.zeros((V,), jnp.float32)}
        return inp
    _L1_cond_all = _L1_cond_setup()
    _L1_cond_in = {k: v for k, v in _L1_cond_all.items() if k in ('Wq', 'Wk', 'Wv', 'Wp', 'bp', 'cW1', 'cb1', 'cW2', 'cb2', 'mW1', 'mb1', 'mW2', 'mb2')}
    del _L1_cond_all

    def _L2_cond_setup():
        import jax, jax.numpy as jnp
        import numpy as np
        H = 256
        K = 128
        R = 3
        B = 8
        S = 256
        LN_EPS = 1e-05
        key = jax.random.key(seed)
        ks = jax.random.split(key, 8)
        sd_d = 1.0 / np.sqrt(H)
        sd_u = 1.0 / np.sqrt(K)
        return {'role': jax.random.randint(ks[0], (B,), 0, R), 'hidden_states': jax.random.normal(ks[1], (B, S, H), dtype=jnp.float32), 'W_down': jax.random.uniform(ks[2], (R, H, K), jnp.float32, -sd_d, sd_d), 'b_down': jax.random.uniform(ks[3], (R, K), jnp.float32, -sd_d, sd_d), 'W_up': jax.random.uniform(ks[4], (R, K, H), jnp.float32, -sd_u, sd_u), 'b_up': jax.random.uniform(ks[5], (R, H), jnp.float32, -sd_u, sd_u), 'gamma': jnp.ones((R, H), jnp.float32), 'beta': jnp.zeros((R, H), jnp.float32)}
    _L2_cond_all = _L2_cond_setup()
    _L2_cond_in = {k: v for k, v in _L2_cond_all.items() if k in ('W_down', 'b_down', 'W_up', 'b_up', 'gamma', 'beta')}
    del _L2_cond_all

    def _L3_cond_setup():
        import jax, jax.numpy as jnp
        import numpy as np
        B, S, H = (8, 256, 256)
        BN = 128
        E = 3
        LN_EPS = 1e-05
        key = jax.random.key(seed)
        ks = jax.random.split(key, 8)
        stream = jax.random.randint(ks[0], (B,), 0, E, dtype=jnp.int32)
        hidden_states = jax.random.normal(ks[1], (B, S, H), dtype=jnp.float32)
        W_down = jax.random.normal(ks[2], (E, H, BN), dtype=jnp.float32) * 0.02
        b_down = jnp.zeros((E, BN), dtype=jnp.float32)
        W_up = jax.random.normal(ks[3], (E, BN, H), dtype=jnp.float32) * 0.02
        b_up = jnp.zeros((E, H), dtype=jnp.float32)
        ln_w = jnp.ones((E, H), dtype=jnp.float32)
        ln_b = jnp.zeros((E, H), dtype=jnp.float32)
        return {'stream': stream, 'hidden_states': hidden_states, 'W_down': W_down, 'b_down': b_down, 'W_up': W_up, 'b_up': b_up, 'ln_w': ln_w, 'ln_b': ln_b}
    _L3_cond_all = _L3_cond_setup()
    _L3_cond_in = {k: v for k, v in _L3_cond_all.items() if k in ('W_down', 'b_down', 'W_up', 'b_up', 'ln_w', 'ln_b')}
    del _L3_cond_all
    return {'x': x, 'itok_B_1_2': itok_B_1_2, 'itok_B_17_1546': itok_B_17_1546, '_lenS': _lenS, 'L0_cond_W_down': _L0_cond_in['W_down'], 'L0_cond_b_down': _L0_cond_in['b_down'], 'L0_cond_W_up': _L0_cond_in['W_up'], 'L0_cond_b_up': _L0_cond_in['b_up'], 'L0_cond_gamma': _L0_cond_in['gamma'], 'L0_cond_beta': _L0_cond_in['beta'], 'L1_cond_Wq': _L1_cond_in['Wq'], 'L1_cond_Wk': _L1_cond_in['Wk'], 'L1_cond_Wv': _L1_cond_in['Wv'], 'L1_cond_Wp': _L1_cond_in['Wp'], 'L1_cond_bp': _L1_cond_in['bp'], 'L1_cond_cW1': _L1_cond_in['cW1'], 'L1_cond_cb1': _L1_cond_in['cb1'], 'L1_cond_cW2': _L1_cond_in['cW2'], 'L1_cond_cb2': _L1_cond_in['cb2'], 'L1_cond_mW1': _L1_cond_in['mW1'], 'L1_cond_mb1': _L1_cond_in['mb1'], 'L1_cond_mW2': _L1_cond_in['mW2'], 'L1_cond_mb2': _L1_cond_in['mb2'], 'L2_cond_W_down': _L2_cond_in['W_down'], 'L2_cond_b_down': _L2_cond_in['b_down'], 'L2_cond_W_up': _L2_cond_in['W_up'], 'L2_cond_b_up': _L2_cond_in['b_up'], 'L2_cond_gamma': _L2_cond_in['gamma'], 'L2_cond_beta': _L2_cond_in['beta'], 'L3_cond_W_down': _L3_cond_in['W_down'], 'L3_cond_b_down': _L3_cond_in['b_down'], 'L3_cond_W_up': _L3_cond_in['W_up'], 'L3_cond_b_up': _L3_cond_in['b_up'], 'L3_cond_ln_w': _L3_cond_in['ln_w'], 'L3_cond_ln_b': _L3_cond_in['ln_b']}

def reference(x, itok_B_1_2, itok_B_17_1546, _lenS, L0_cond_W_down, L0_cond_b_down, L0_cond_W_up, L0_cond_b_up, L0_cond_gamma, L0_cond_beta, L1_cond_Wq, L1_cond_Wk, L1_cond_Wv, L1_cond_Wp, L1_cond_bp, L1_cond_cW1, L1_cond_cb1, L1_cond_cW2, L1_cond_cb2, L1_cond_mW1, L1_cond_mb1, L1_cond_mW2, L1_cond_mb2, L2_cond_W_down, L2_cond_b_down, L2_cond_W_up, L2_cond_b_up, L2_cond_gamma, L2_cond_beta, L3_cond_W_down, L3_cond_b_down, L3_cond_W_up, L3_cond_b_up, L3_cond_ln_w, L3_cond_ln_b):
    import jax
    import jax.numpy as jnp

    def _L0_cond_ref(role, hidden_states, W_down, b_down, W_up, b_up, gamma, beta):
        import jax, jax.numpy as jnp
        import numpy as np
        H = 256
        K = 128
        R = 3
        B = 8
        S = 256
        LN_EPS = 1e-05
        h = jnp.einsum('bsh,bhk->bsk', hidden_states, W_down[role]) + b_down[role][:, None, :]
        h = jax.nn.gelu(h, approximate=False)
        u = jnp.einsum('bsk,bkh->bsh', h, W_up[role]) + b_up[role][:, None, :]
        y = hidden_states + u
        mean = jnp.mean(y, axis=-1, keepdims=True)
        var = jnp.mean(jnp.square(y - mean), axis=-1, keepdims=True)
        yn = (y - mean) * jax.lax.rsqrt(var + LN_EPS)
        return yn * gamma[role][:, None, :] + beta[role][:, None, :]

    def _L1_cond_ref(x, lens, target_codes, Wq, Wk, Wv, Wp, bp, cW1, cb1, cW2, cb2, mW1, mb1, mW2, mb2):
        import jax, jax.numpy as jnp
        import numpy as np
        B, T, V = (8, 64, 256)
        H = 4 * V
        scale = V ** (-0.5)
        q = x @ Wq
        k = x @ Wk
        v = x @ Wv
        attn = jnp.einsum('btd,bTd->btT', q, k) * scale
        attn = jax.nn.softmax(attn, axis=-1)
        attn_out = jnp.einsum('btT,bTd->btd', attn, v) @ Wp + bp
        target_embed = jax.nn.one_hot(target_codes, V, dtype=x.dtype)[:, None, :]
        cms_out = jax.nn.gelu(attn_out @ cW1 + cb1, approximate=False) @ cW2 + cb2
        cms_out = cms_out + target_embed
        concat = jnp.concatenate([attn_out, cms_out], axis=-1)
        modifier = jax.nn.gelu(concat @ mW1 + mb1, approximate=False) @ mW2 + mb2
        out = jnp.clip(x + cms_out + modifier, 0.0, 1.0)
        return out

    def _L2_cond_ref(role, hidden_states, W_down, b_down, W_up, b_up, gamma, beta):
        import jax, jax.numpy as jnp
        import numpy as np
        H = 256
        K = 128
        R = 3
        B = 8
        S = 256
        LN_EPS = 1e-05
        h = jnp.einsum('bsh,bhk->bsk', hidden_states, W_down[role]) + b_down[role][:, None, :]
        h = jax.nn.gelu(h, approximate=False)
        u = jnp.einsum('bsk,bkh->bsh', h, W_up[role]) + b_up[role][:, None, :]
        y = hidden_states + u
        mean = jnp.mean(y, axis=-1, keepdims=True)
        var = jnp.mean(jnp.square(y - mean), axis=-1, keepdims=True)
        yn = (y - mean) * jax.lax.rsqrt(var + LN_EPS)
        return yn * gamma[role][:, None, :] + beta[role][:, None, :]

    def _L3_cond_ref(stream, hidden_states, W_down, b_down, W_up, b_up, ln_w, ln_b):
        import jax, jax.numpy as jnp
        import numpy as np
        B, S, H = (8, 256, 256)
        BN = 128
        E = 3
        LN_EPS = 1e-05
        Wd = W_down[stream]
        bd = b_down[stream]
        Wu = W_up[stream]
        bu = b_up[stream]
        g = ln_w[stream]
        b = ln_b[stream]
        residual = hidden_states
        h = jnp.einsum('bsh,bhk->bsk', hidden_states, Wd) + bd[:, None, :]
        h = jax.nn.gelu(h, approximate=False)
        h = jnp.einsum('bsk,bkh->bsh', h, Wu) + bu[:, None, :]
        h = residual + h
        mean = jnp.mean(h, axis=-1, keepdims=True)
        var = jnp.mean(jnp.square(h - mean), axis=-1, keepdims=True)
        h = (h - mean) * jax.lax.rsqrt(var + LN_EPS)
        return h * g[:, None, :] + b[:, None, :]
    x = _L0_cond_ref(itok_B_1_2, x, L0_cond_W_down, L0_cond_b_down, L0_cond_W_up, L0_cond_b_up, L0_cond_gamma, L0_cond_beta)
    x = _L1_cond_ref(x, _lenS, itok_B_17_1546, L1_cond_Wq, L1_cond_Wk, L1_cond_Wv, L1_cond_Wp, L1_cond_bp, L1_cond_cW1, L1_cond_cb1, L1_cond_cW2, L1_cond_cb2, L1_cond_mW1, L1_cond_mb1, L1_cond_mW2, L1_cond_mb2)
    x = _L2_cond_ref(itok_B_1_2, x, L2_cond_W_down, L2_cond_b_down, L2_cond_W_up, L2_cond_b_up, L2_cond_gamma, L2_cond_beta)
    x = _L3_cond_ref(itok_B_1_2, x, L3_cond_W_down, L3_cond_b_down, L3_cond_W_up, L3_cond_b_up, L3_cond_ln_w, L3_cond_ln_b)
    return x

_drawn_inputs = setup_inputs


def setup_inputs(seed=0):
    import zlib

    import numpy as np

    out = dict(_drawn_inputs(seed))
    spreads = {'L0_cond_gamma': (1.0, 0.2),
     'L0_cond_beta': (0.0, 0.1),
     'L1_cond_bp': (0.0, 0.1),
     'L1_cond_cb1': (0.0, 0.1),
     'L1_cond_cb2': (0.0, 0.1),
     'L1_cond_mb1': (0.0, 0.1),
     'L1_cond_mb2': (0.0, 0.1),
     'L2_cond_gamma': (1.0, 0.2),
     'L2_cond_beta': (0.0, 0.1),
     'L3_cond_b_down': (0.0, 0.68),
     'L3_cond_b_up': (0.0, 0.1),
     'L3_cond_ln_w': (1.0, 0.2),
     'L3_cond_ln_b': (0.0, 0.1)}
    factors = {'L0_cond_b_down': 3.024}
    for name, (base, spread) in spreads.items():
        noise = np.random.default_rng([zlib.crc32(name.encode()), seed]).standard_normal(out[name].shape)
        drawn = base * np.exp(spread * noise) if base else spread * noise
        out[name] = jnp.asarray(drawn.astype(out[name].dtype))
    for name, factor in factors.items():
        out[name] = (out[name] * factor).astype(out[name].dtype)
    return out
```

```python
from contextlib import ExitStack

import concourse.bass as bass
from concourse import mybir

F32 = mybir.dt.float32
F32R = mybir.dt.float32r
I32 = mybir.dt.int32
U32 = mybir.dt.uint32
ALU = mybir.AluOpType
ACT = mybir.ActivationFunctionType
X_AXIS = mybir.AxisListType.X

P = 128
B, S, D = 32, 32, 256
N = B * S
R = 3
KD = D // P
HID = 4 * D
JT = HID // P
HALF = N // 2
G = HALF // P
WB = P // S
CHUNKS = (B + R * (WB - 1)) // WB
POS = B + WB
LN_EPS = 1e-5
SCALE = float(D) ** -0.5

BD, GAMMA0, BETA0, GAMMA2, BETA2 = (0, 1, 2), 3, 5, 7, 9
PER_ROLE = 11
BP = PER_ROLE * R
CB1, CB2 = BP + KD, BP + KD + JT
MB1, MB2 = CB2 + KD, CB2 + KD + JT
ROWS = MB2 + KD

XSLOTS, YSLOTS, WSLOTS = 2, 3, 4
STAGE = 3
ADAPTER_BANKS = 4
CHAIN_BANKS = (5, 6, 7, 5, 6, 7, 4, 3, 2, 5)
RING = (2, 3, 4)


def plan():
    steps = [("vectors",), ("order",), ("fold_transpose",), ("fold",)]

    def tick0(t):
        for name, c in (("norm0", t - 3), ("up", t - 2), ("down", t - 1), ("load0", t)):
            if 0 <= c < CHUNKS:
                steps.append((name, c) if name in ("norm0", "load0") else (name, 0, c))

    def chain_tick(t, chunks, every):
        stages = ("load2", "down2", "up2", "norm2", "down3", "up3", "norm3")
        for c in chunks:
            k = t - every * (c - chunks[0])
            if 0 <= k < len(stages):
                name = stages[k]
                if name in ("down2", "up2"):
                    steps.append((name[:-1], 2, c))
                elif name in ("down3", "up3"):
                    steps.append((name[:-1], 3, c))
                else:
                    steps.append((name, c))

    weights = [("weights", p) for p in range(4)]
    for t in range(9):
        tick0(t)
        if t >= 4 and t < 8:
            steps.append(weights[t - 4])
    steps += [("tokens", 0), ("project", 0)]
    tick0(9)
    steps += [("scores", 0)]
    tick0(10)
    tick0(11)
    steps += [("mix", 0)]
    tick0(12)
    steps += [("tokens", 1), ("project", 1), ("attend", 0), ("scores", 1)]
    steps += [("hidden", 0, j) for j in range(4)]
    steps += [("mix", 1), ("tables",)]
    steps += [("hidden", 0, j) for j in range(4, 6)]
    steps += [("attend", 1)]
    steps += [("hidden", 0, j) for j in range(6, 8)]
    steps += [("weights", 4), ("outer", 0), ("weights", 5)]
    for j in range(JT):
        steps.append(("hidden", 1, j))
        if j in (1, 4):
            steps.append(("weights", 6 + (j == 4)))
    steps += [("outer", 1), ("weights", 8)]
    for j in range(JT):
        steps.append(("hidden", 2, j))
        if j == 3:
            steps.append(("weights", 9))
    steps += [("outer", 2)]
    first = list(range(4))
    for j in range(JT):
        steps.append(("hidden", 3, j))
        chain_tick(j, first, 2)
    steps += [("outer", 3, 0)]
    for t in range(JT, 6 + 2 * 3 + 1):
        chain_tick(t, first, 2)
        if t - JT + 1 < 4:
            steps.append(("outer", 3, t - JT + 1))
    rest = list(range(4, CHUNKS))
    for t in range(6 + 2 * (len(rest) - 1) + 1):
        chain_tick(t, rest, 2)
    return steps


def build(nc, a, out):
    steps = plan()
    with ExitStack() as ctx:
        at = [(nc.sbuf_base + 31) // 32 * 32]

        def place(name, shape, dt, offset=None):
            size = 4
            for n in shape[1:]:
                size *= n
            size = (size + 31) // 32 * 32
            if offset is None:
                offset = at[0]
                at[0] += size
            return nc.alloc_sbuf_tensor_at(name, shape, dt, offset=offset)

        def sem(name):
            return ctx.enter_context(nc.semaphore(name))

        bank = [ctx.enter_context(nc.psum_tensor(f"bank{b}", [P, 512], F32)) for b in range(8)]

        ident = place("ident", [P, P], F32)
        pos_row = place("pos_row", [P, POS], F32)
        chunk4_row = place("chunk4_row", [P, CHUNKS], F32)
        role_row = place("role_row", [P, R, B], F32)
        four_row = place("four_row", [P, R, 8], F32)
        role_in = place("role_in", [P, CHUNKS, R], F32)
        part_col = place("part_col", [P, 1], F32)
        part_col2 = place("part_col2", [P, 1], F32)
        seq_col = place("seq_col", [P, 1], F32)
        seq_from = place("seq_from", [P, WB - 1], F32)
        past = place("past", [P, WB - 1], F32)
        spare_col = place("spare_col", [P, 1], F32)
        tok_spare = place("tok_spare", [P, 1], F32)
        power = place("power", [P, 1], F32)
        roles_i = place("roles_i", [P, B], I32)
        role_col_i = place("role_col_i", [B, 2], I32)
        roles = place("roles", [P, B], F32)
        keys = place("keys", [P, B], F32)
        key_col = place("key_col", [B, 2], F32)
        below = place("below", [B, B], F32)
        pos_col = place("pos_col", [B, 1], F32)
        sorts = place("sorts", [B, POS], F32)
        spread = place("spread", [B, 2, P], F32)
        is_role = place("is_role", [P, R, B], F32)
        count = place("count", [P, R], F32)
        more = place("more", [P, R, 8], F32)
        wins = place("wins", [P, R], F32)
        ends4 = place("ends4", [P, 2], F32)
        short = place("short", [P, 2], F32)
        later = place("later", [P, 2, CHUNKS], F32)
        chunk_role = place("chunk_role", [P, CHUNKS], F32)
        start = place("start", [P, CHUNKS], F32)
        end = place("end", [P, CHUNKS], F32)
        start_tok_i = place("start_tok_i", [P, CHUNKS], I32)
        chunk_role_i = place("chunk_role_i", [P, CHUNKS], I32)
        order = place("order", [P, 2, POS], F32)
        reach = place("reach", [P, CHUNKS, POS], F32)
        seq_at = place("seq_at", [P, CHUNKS], F32)
        seq_at_i = place("seq_at_i", [P, CHUNKS], I32)
        valid = place("valid", [P, CHUNKS], F32)
        row_at = place("row_at", [P, CHUNKS], F32)
        row_at_i = place("row_at_i", [P, CHUNKS], U32)
        role_hot = place("role_hot", [P, CHUNKS, R], F32)
        vec_rows = place("vec_rows", [ROWS, P], F32)
        vecs = place("vecs", [P, ROWS], F32)
        picked = place("picked", [P, PER_ROLE, CHUNKS, R], F32)
        chunk_vecs = place("chunk_vecs", [P, PER_ROLE, CHUNKS], F32)
        target = place("target", [P, KD, POS], F32)

        stage = [place(f"stage{i}", [P, HID], F32) for i in range(STAGE)]
        wdA = [place(f"wdA{i}", [P, KD, P], F32) for i in range(WSLOTS)]
        wuA = [place(f"wuA{i}", [P, D], F32) for i in range(WSLOTS)]
        wdB = [place(f"wdB{i}", [P, KD, P], F32) for i in range(YSLOTS)]
        wuB = [place(f"wuB{i}", [P, D], F32) for i in range(YSLOTS)]
        xA = [place(f"xA{i}", [P, KD, P], F32) for i in range(XSLOTS)]
        hA = [place(f"hA{i}", [P, P], F32) for i in range(XSLOTS)]
        yA = [place(f"yA{i}", [P, D], F32) for i in range(YSLOTS)]
        zB = [place(f"zB{i}", [P, KD, P], F32) for i in range(XSLOTS)]
        hB = [place(f"hB{i}", [P, P], F32) for i in range(XSLOTS)]
        yB = [place(f"yB{i}", [P, D], F32) for i in range(YSLOTS)]
        statsA = place("statsA", [P, YSLOTS, 6], F32)
        mvA = place("mvA", [P, YSLOTS, 2], F32)
        rstdA = place("rstdA", [P, YSLOTS, 2], F32)
        statsB = place("statsB", [P, YSLOTS, 6], F32)
        mvB = place("mvB", [P, YSLOTS, 2], F32)
        rstdB = place("rstdB", [P, YSLOTS, 2], F32)
        table = {}
        for name in ("bu2", "gamma2", "beta2", "gamma3", "beta3"):
            table[name] = place(f"table_{name}", [P, R, D], F32)
        x1T = place("x1T", [P, KD, POS * S], F32)
        cw1_at = at[0]
        cw1 = [place(f"cw1_{x}", [P, KD, HID], F32R) for x in "hl"]
        cw2 = [place(f"cw2_{x}", [P, JT, D], F32R) for x in "hl"]
        mw2 = [place(f"mw2_{x}", [P, JT, D], F32R, cw1_at + n * 4 * JT * D) for n, x in enumerate("hl")]
        ao = [[place(f"ao{h}_{x}", [P, KD, HALF], F32R) for x in "hl"] for h in range(2)]
        g = [place(f"g_{x}", [P, JT, HALF], F32R) for x in "hl"]
        g_full = [place(f"g_full{i}", [P, HALF], F32) for i in range(2)]

        early = at[0]
        for name in ("bu0", "bu3"):
            table[name] = place(f"table_{name}", [P, R, D], F32)
        x_tok = [place(f"x_tok{i}", [P, D], F32) for i in range(4)]
        wT = {w: place(f"wT_{w}", [P, KD, D], F32) for w in "qkv"}
        wqk = [place(f"wqk_{x}", [P, KD, D], F32R) for x in "hl"]
        wvp = [place(f"wvp_{x}", [P, KD, D], F32R) for x in "hl"]
        x1 = [place(f"x1_{x}", [P, KD, HALF], F32R) for x in "hl"]
        y_T = place("y_T", [P, KD, HALF], F32)
        x1_tok = place("x1_tok", [P, G, D], F32)
        probs_T = place("probs_T", [P, G, P], F32)
        dots = place("dots", [P, G, S], F32)
        weighed = place("weighed", [P, G, S], F32)
        probs = place("probs", [P, G, S], F32)
        peak = place("peak", [P, G], F32)
        total = place("total", [P, G], F32)
        inv_total = place("inv_total", [P, G], F32)
        z = [place(f"z_{x}", [P, KD, HALF], F32R) for x in "hl"]
        early_end = at[0]

        at[0] = early
        mw1 = [place(f"mw1_{x}", [P, 2 * KD, HID], F32R) for x in "hl"]
        cms = [[place(f"cms{h}_{x}", [P, KD, HALF], F32R) for x in "hl"] for h in range(2)]
        cms_full = place("cms_full", [P, KD, HALF], F32)
        at[0] = max(at[0], early_end)

        ids_in = sem("ids_in")
        vectors_in = sem("vectors_in")
        table0_in = sem("table0_in")
        tables_in = sem("tables_in")
        stage_in = [sem(f"stage_in{i}") for i in range(STAGE)]
        wA_in = [sem(f"wA_in{i}") for i in range(WSLOTS)]
        wB_in = [sem(f"wB_in{i}") for i in range(YSLOTS)]
        x_in = [sem(f"x_in{i}") for i in range(4)]
        out_done = [sem(f"out_done{i}") for i in range(YSLOTS)]
        constants = sem("constants")
        dve_own = sem("dve_own")
        pool_own = sem("pool_own")
        sorts_ready = sem("sorts_ready")
        order_ps = sem("order_ps")
        chunks_ready = sem("chunks_ready")
        seqs_ready = sem("seqs_ready")
        rows_ready = sem("rows_ready")
        vectors_ps = sem("vectors_ps")
        vectors_ready = sem("vectors_ready")
        chunk_vecs_ready = sem("chunk_vecs_ready")
        target_ready = sem("target_ready")
        beta_ready = sem("beta_ready")
        wT_ps = sem("wT_ps")
        wT_ready = sem("wT_ready")
        fold_ps = sem("fold_ps")
        fold_high = sem("fold_high")
        fold_ready = sem("fold_ready")
        w_high = sem("w_high")
        w_ready = sem("w_ready")
        order_ready = sem("order_ready")
        sumA_ready = sem("sumA_ready")
        sumB_ready = sem("sumB_ready")
        dots_copied = sem("dots_copied")
        x2_sum = sem("x2_sum")
        xT_ps = sem("xT_ps")
        xA_ready = sem("xA_ready")
        resA_ready = sem("resA_ready")
        downA_ps = sem("downA_ps")
        hA_ready = sem("hA_ready")
        upA_ps = sem("upA_ps")
        varA_ready = sem("varA_ready")
        rstdA_ready = sem("rstdA_ready")
        normA_ready = sem("normA_ready")
        normA_T_ps = sem("normA_T_ps")
        x1_window = sem("x1_window")
        zB_ready = sem("zB_ready")
        resB_half = sem("resB_half")
        resB_ready = sem("resB_ready")
        downB_ps = sem("downB_ps")
        hB_ready = sem("hB_ready")
        upB_ps = sem("upB_ps")
        varB_ready = sem("varB_ready")
        rstdB_ready = sem("rstdB_ready")
        out_ready = sem("out_ready")
        tokens_ps = sem("tokens_ps")
        tokens_ready = sem("tokens_ready")
        x1_split = sem("x1_split")
        project_ps = sem("project_ps")
        y_ready = sem("y_ready")
        scores_ps = sem("scores_ps")
        dots_ready = sem("dots_ready")
        exp_ready = sem("exp_ready")
        probs_ready = sem("probs_ready")
        mix_ps = sem("mix_ps")
        z_high = sem("z_high")
        z_ready = sem("z_ready")
        attend_ps = sem("attend_ps")
        ao_high = sem("ao_high")
        ao_ready = sem("ao_ready")
        hidden_ps = sem("hidden_ps")
        g_high = sem("g_high")
        g_ready = sem("g_ready")
        outer_ps = sem("outer_ps")
        cms_full_ready = sem("cms_full_ready")
        cms_high = sem("cms_high")
        cms_ready = sem("cms_ready")
        sum_ready = sem("sum_ready")
        x2_ready = sem("x2_ready")

        def lane_a(layer, c):
            return c if layer == 0 else CHUNKS + c

        def chain_bank(layer, c):
            return ADAPTER_BANKS + c % 4 if layer == 0 else CHAIN_BANKS[c]

        def rows(w, t):
            return a[w][t * P:(t + 1) * P, :]

        def four_tiles(w, t):
            return a[w][t * 4 * P:(t + 1) * 4 * P, :].rearrange("(k p) n -> p k n", p=P)

        def wide(slot):
            return stage[slot][:, :]

        def tiled(slot):
            return stage[slot][:, :].rearrange("p (k n) -> p k n", n=D)

        pieces = []
        for t in range(KD):
            pieces.append((rows("L1_cond_cW1", t), wide, [w[:, t, :] for w in cw1]))
        for t in range(2):
            pieces.append((four_tiles("L1_cond_cW2", t), tiled, [w[:, 4 * t:4 * t + 4, :] for w in cw2]))
        for t in range(2 * KD):
            pieces.append((rows("L1_cond_mW1", t), wide, [w[:, t, :] for w in mw1]))
        for t in range(2):
            pieces.append((four_tiles("L1_cond_mW2", t), tiled, [w[:, 4 * t:4 * t + 4, :] for w in mw2]))

        def filling(p):
            return (p + 2) % STAGE, (p + 2) // STAGE + 1

        down_w = {0: "L0_cond_W_down", 2: "L2_cond_W_down", 3: "L3_cond_W_down"}
        up_w = {0: "L0_cond_W_up", 2: "L2_cond_W_up", 3: "L3_cond_W_up"}

        block = ctx.enter_context(nc.Block())

        @block.sync
        def _(sp):
            sp.dma_start(roles_i[:, :], a["itok_B_1_2"].partition_broadcast(P)).then_inc(ids_in, 16)
            sp.dma_start(role_col_i[:, 0:1], a["itok_B_1_2"].rearrange("(b o) -> b o", o=1)).then_inc(ids_in, 16)
            sp.dma_start(role_col_i[:, 1:2], a["itok_B_17_1546"].rearrange("(b o) -> b o", o=1)).then_inc(ids_in, 16)
            for n, pair in enumerate((("L1_cond_Wq", "L1_cond_Wk"), ("L1_cond_Wv", "L1_cond_Wp"))):
                for m, w in enumerate(pair):
                    sp.dma_start(tiled(n)[:, KD * m:KD * (m + 1), :],
                                 a[w].rearrange("(k p) n -> p k n", p=P)).then_inc(stage_in[n], 16)

            def piece(p):
                slot, _ = filling(p)
                src, view, _ = pieces[p]
                if p == 1:
                    sp.wait_ge(wT_ps, 2)
                elif p == 2:
                    sp.wait_ge(fold_ps, KD)
                elif p > 2:
                    sp.wait_ge(w_ready, p - STAGE + 1)
                sp.dma_start(view(slot), src).then_inc(stage_in[slot], 16)

            def adapter_weights(layer, c):
                if layer == 3:
                    slot, down, up, done = c % YSLOTS, wdB, wuB, wB_in
                    if c >= YSLOTS:
                        sp.wait_ge(upB_ps, c - YSLOTS + 1)
                else:
                    i = lane_a(layer, c)
                    slot, down, up, done = i % WSLOTS, wdA, wuA, wA_in
                    if i >= WSLOTS:
                        sp.wait_ge(upA_ps, i - WSLOTS + 1)
                r = sp.value_load(chunk_role_i[0:1, c:c + 1], min_val=0, max_val=R - 1)
                sp.dma_start(down[slot][:, :, :],
                             a[down_w[layer]].rearrange("r (k p) n -> r p k n", p=P)[bass.ds(r, 1), :, :, :].rearrange("r p k n -> (r p) k n")).then_inc(done[slot], 16)
                sp.dma_start(up[slot][:, :],
                             a[up_w[layer]][bass.ds(r, 1), :, :].rearrange("r p n -> (r p) n")).then_inc(done[slot], 16)

            def tokens_in(c):
                if c >= 4:
                    sp.wait_ge(upA_ps, c - 3)
                    sp.wait_ge(resA_ready, c - 3)
                for j in range(WB):
                    b = sp.value_load(seq_at_i[S * j:S * j + 1, c:c + 1], min_val=0, max_val=B - 1)
                    sp.dma_start(x_tok[c % 4][S * j:S * (j + 1), :],
                                 a["x"][bass.ds(b, 1), :, :].rearrange("b s d -> (b s) d")).then_inc(x_in[c % 4], 16)

            def table_in(name, w, done):
                sp.dma_start(table[name][:, :, :], a[w].partition_broadcast(P)).then_inc(done, 16)

            piece(0)
            table_in("bu0", "L0_cond_b_up", table0_in)
            sp.wait_ge(chunks_ready, 1)
            adapter_weights(0, 0)
            sp.wait_ge(seqs_ready, 1)
            tokens_in(0)
            for c in range(1, 4):
                tokens_in(c)
                adapter_weights(0, c)
            piece(1)
            piece(2)
            for c in range(4, CHUNKS):
                tokens_in(c)
                adapter_weights(0, c)
                if c == 7:
                    piece(3)
            for name, w in (("bu2", "L2_cond_b_up"), ("gamma2", "L2_cond_gamma"), ("beta2", "L2_cond_beta"),
                            ("gamma3", "L3_cond_ln_w"), ("beta3", "L3_cond_ln_b"), ("bu3", "L3_cond_b_up")):
                table_in(name, w, tables_in)
            for c in range(WSLOTS):
                adapter_weights(2, c)
            for c in range(YSLOTS):
                adapter_weights(3, c)
            for p in range(4, len(pieces)):
                piece(p)
            for c in range(YSLOTS, CHUNKS):
                adapter_weights(3, c)
                if c + 1 < CHUNKS:
                    adapter_weights(2, c + 1)

        @block.tensor
        def _(pe):
            read = [None] * 8

            def take(b, done, value):
                if read[b]:
                    pe.wait_ge(*read[b])
                read[b] = (done, value)

            def split_matmul(dst, w, x, first, last):
                pe.matmul(dst, w[0], x[0], start=first, stop=False)
                pe.matmul(dst, w[0], x[1], start=False, stop=False)
                return pe.matmul(dst, w[1], x[0], start=False, stop=last)

            def vectors():
                pe.wait_ge(constants, 1)
                pe.wait_ge(vectors_in, 16 * 16)
                take(0, vectors_ready, 1)
                pe.transpose(bank[0][:, 0:ROWS], vec_rows[:, :], ident[0:ROWS, 0:ROWS]).then_inc(vectors_ps, 1)

            def find_order():
                pe.wait_ge(sorts_ready, 1)
                take(1, order_ready, 1)
                for n in range(2):
                    mm = pe.matmul(bank[1][:, n * POS:(n + 1) * POS], spread[:, n, :], sorts[:, :],
                                   start=True, stop=True)
                mm.then_inc(order_ps, 1)

            def fold_transpose():
                for n, (slot, half) in enumerate(((0, 0), (0, 1), (1, 0))):
                    pe.wait_ge(stage_in[slot], 32)
                    take(2 + n, wT_ready, n + 1)
                    for i in range(KD):
                        for t in range(KD):
                            tr = pe.transpose(bank[2 + n][:, t * D + i * P:t * D + (i + 1) * P],
                                              tiled(slot)[:, KD * half + i, t * P:(t + 1) * P], ident[:, :])
                    tr.then_inc(wT_ps, 1)

            def fold():
                for n, (left, right) in enumerate((("q", "k"), ("v", None))):
                    take(5 + n, fold_ready, n + 1)
                    pe.wait_ge(wT_ready, 2 + n)
                    for m in range(KD):
                        for t in range(KD):
                            moving = wT[right][:, t, :] if right else tiled(1)[:, KD + t, :]
                            mm = pe.matmul(bank[5 + n][:, m * D:(m + 1) * D], wT[left][:, t, m * P:(m + 1) * P],
                                           moving, start=(t == 0), stop=(t == KD - 1))
                    mm.then_inc(fold_ps, 1)

            def load0(c):
                b = chain_bank(0, c)
                take(b, x1_window, KD * (c + 1))
                pe.wait_ge(x_in[c % 4], 16 * WB * (c // 4 + 1))
                for m in range(KD):
                    tr = pe.transpose(bank[b][:, m * P:(m + 1) * P], x_tok[c % 4][:, m * P:(m + 1) * P], ident[:, :])
                tr.then_inc(xT_ps, 1)

            def load2(c):
                b = chain_bank(2, c)
                take(b, sumB_ready, c + 1)
                i = lane_a(2, c)
                pe.wait_ge(xA_ready, i + 1)
                for m in range(KD):
                    tr = pe.transpose(bank[b][:, m * P:(m + 1) * P], xA[i % XSLOTS][:, m, :], ident[:, :])
                tr.then_inc(xT_ps, 1)

            def down(layer, c):
                dst = bank[chain_bank(layer, c)][:, D:D + P]
                if layer == 3:
                    pe.wait_ge(wB_in[c % YSLOTS], 32 * (c // YSLOTS + 1))
                    pe.wait_ge(zB_ready, c + 1)
                    w, x, done = wdB[c % YSLOTS], zB[c % XSLOTS], downB_ps
                else:
                    i = lane_a(layer, c)
                    pe.wait_ge(wA_in[i % WSLOTS], 32 * (i // WSLOTS + 1))
                    pe.wait_ge(xA_ready, i + 1)
                    if layer == 2:
                        pe.wait_ge(resA_ready, i + 1)
                    w, x, done = wdA[i % WSLOTS], xA[i % XSLOTS], downA_ps
                for k in range(KD):
                    mm = pe.matmul(dst, w[:, k, :], x[:, k, :], start=(k == 0), stop=(k == KD - 1))
                mm.then_inc(done, 1)

            def up(layer, c):
                dst = bank[chain_bank(layer, c)][:, 0:D]
                if layer == 3:
                    pe.wait_ge(hB_ready, c + 1)
                    pe.matmul(dst, hB[c % XSLOTS][:, :], wuB[c % YSLOTS][:, :], start=True, stop=True).then_inc(upB_ps, 1)
                else:
                    i = lane_a(layer, c)
                    pe.wait_ge(hA_ready, i + 1)
                    pe.matmul(dst, hA[i % XSLOTS][:, :], wuA[i % WSLOTS][:, :], start=True, stop=True).then_inc(upA_ps, 1)

            def norm(layer, c):
                b, i = chain_bank(layer, c), lane_a(layer, c)
                pe.wait_ge(normA_ready, i + 1)
                for m in range(KD):
                    tr = pe.transpose(bank[b][:, m * P:(m + 1) * P], yA[i % YSLOTS][:, m * P:(m + 1) * P], ident[:, :])
                tr.then_inc(normA_T_ps, 1)

            def windows_done(h):
                pe.wait_ge(x1_window, KD * (6 if h == 0 else CHUNKS))

            def tokens(h):
                windows_done(h)
                for q in range(2):
                    take(2 + q, tokens_ready, 2 * h + q + 1)
                    for n in range(2):
                        for m in range(KD):
                            lo = h * HALF + (2 * q + n) * P
                            tr = pe.transpose(bank[2 + q][:, n * D + m * P:n * D + (m + 1) * P],
                                              x1T[:, m, lo:lo + P], ident[:, :])
                    tr.then_inc(tokens_ps, 1)

            def pair(w, x, done, read_by, h):
                for m in range(KD):
                    take(m, read_by, KD * h + m + 1)
                    for k in range(KD):
                        mm = split_matmul(bank[m][:, :], [v[:, k, m * P:(m + 1) * P] for v in w],
                                          [v[:, k, :] for v in x], k == 0, k == KD - 1)
                    mm.then_inc(done, 1)

            def project(h):
                pe.wait_ge(fold_ready, 1)
                pe.wait_ge(x1_split, h + 1)
                pair(wqk, x1, project_ps, y_ready, h)

            def scores(h):
                pe.wait_ge(y_ready, KD * (h + 1))
                take(2, dots_copied, h + 1)
                for n in range(G):
                    for k in range(KD):
                        mm = pe.matmul(bank[2][:, n * P:(n + 1) * P], y_T[:, k, n * P:(n + 1) * P],
                                       x1T[:, k, h * HALF + n * P:h * HALF + (n + 1) * P],
                                       start=(k == 0), stop=(k == KD - 1))
                mm.then_inc(scores_ps, 1)

            def mix(h):
                pe.wait_ge(tokens_ready, 2 * (h + 1))
                pe.wait_ge(probs_ready, h + 1)
                for m in range(KD):
                    take(m, z_ready, KD * h + m + 1)
                    for n in range(G):
                        mm = pe.matmul(bank[m][:, n * P:(n + 1) * P], x1_tok[:, n, m * P:(m + 1) * P],
                                       probs_T[:, n, :], start=True, stop=True)
                    mm.then_inc(mix_ps, 1)

            def attend(h):
                pe.wait_ge(fold_ready, 2)
                pe.wait_ge(z_ready, KD * (h + 1))
                pair(wvp, z, attend_ps, ao_ready, h)

            def hidden(phase, j):
                h, n = phase % 2, phase * JT + j
                b = RING[n % len(RING)]
                take(b, g_high, n + 1)
                if phase < 2:
                    pe.wait_ge(w_ready, KD)
                    pe.wait_ge(ao_ready, KD * (h + 1))
                    w, x = cw1, [(ao[h], k) for k in range(KD)]
                else:
                    pe.wait_ge(w_ready, 8)
                    pe.wait_ge(cms_ready, KD * (h + 1))
                    w, x = mw1, [(ao[h], k) for k in range(KD)] + [(cms[h], k) for k in range(KD)]
                for k, (v, kk) in enumerate(x):
                    mm = split_matmul(bank[b][:, :], [u[:, k, j * P:(j + 1) * P] for u in w],
                                      [u[:, kk, :] for u in v], k == 0, k == len(x) - 1)
                mm.then_inc(hidden_ps, 1)

            def outer(phase, part=None):
                w = cw2 if phase < 2 else mw2
                if part in (None, 0):
                    for m in range(KD):
                        if phase < 2:
                            take(m, cms_full_ready, KD * phase + m + 1)
                        else:
                            take(m, x2_sum, KD * (phase - 2) + m + 1)
                    pe.wait_ge(w_ready, 4 if phase < 2 else 10)
                tiles = range(JT) if part is None else range(2 * part, 2 * part + 2)
                for k in tiles:
                    pe.wait_ge(g_ready, phase * JT + k + 1)
                    for m in range(KD):
                        mm = split_matmul(bank[m][:, :], [v[:, k, m * P:(m + 1) * P] for v in w],
                                          [v[:, k, :] for v in g], k == 0, k == JT - 1)
                        if k == JT - 1:
                            mm.then_inc(outer_ps, 1)

            do = {"vectors": vectors, "order": find_order, "fold_transpose": fold_transpose, "fold": fold,
                  "load0": load0, "load2": load2, "down": down, "up": up,
                  "norm0": lambda c: norm(0, c), "norm2": lambda c: norm(2, c),
                  "tokens": tokens, "project": project, "scores": scores, "mix": mix, "attend": attend,
                  "hidden": hidden, "outer": outer}
            for name, *args in steps:
                if name in do:
                    do[name](*args)

        @block.scalar
        def _(act):
            for kind, w in enumerate(("L0_cond_b_down", "L2_cond_b_down", "L3_cond_b_down")):
                act.dma_start(vec_rows[R * kind:R * (kind + 1), :], a[w]).then_inc(vectors_in, 16)
            for v, w in ((GAMMA0, "L0_cond_gamma"), (BETA0, "L0_cond_beta"), (GAMMA2, "L2_cond_gamma"),
                         (BETA2, "L2_cond_beta")):
                for m in range(KD):
                    act.dma_start(vec_rows[R * (v + m):R * (v + m + 1), :],
                                  a[w][:, m * P:(m + 1) * P]).then_inc(vectors_in, 16)
            for row, w, n in ((BP, "L1_cond_bp", KD), (CB1, "L1_cond_cb1", JT), (CB2, "L1_cond_cb2", KD),
                              (MB1, "L1_cond_mb1", JT), (MB2, "L1_cond_mb2", KD)):
                act.dma_start(vec_rows[row:row + n, :], a[w].rearrange("(n p) -> n p", p=P)).then_inc(vectors_in, 16)

            def vectors():
                act.wait_ge(vectors_ps, 1)
                act.copy(vecs[:, :], bank[0][:, 0:ROWS]).then_inc(vectors_ready, 1)

            def find_order():
                act.wait_ge(order_ps, 1)
                act.copy(order[:, :, :].rearrange("p a b -> p (a b)"), bank[1][:, 0:2 * POS]).then_inc(order_ready, 1)

            def fold_transpose():
                for n, w in enumerate("qkv"):
                    act.wait_ge(wT_ps, n + 1)
                    act.copy(wT[w][:, :, :].rearrange("p t n -> p (t n)"), bank[2 + n][:, :]).then_inc(wT_ready, 1)

            def fold():
                for n, w in enumerate((wqk, wvp)):
                    act.wait_ge(fold_ps, n + 1)
                    act.copy(w[0][:, :, :].rearrange("p k n -> p (k n)"), bank[5 + n][:, :]).then_inc(fold_high, 1)

            def load0(c):
                act.wait_ge(xT_ps, c + 1)
                if c >= XSLOTS:
                    act.wait_ge(downA_ps, c - XSLOTS + 1)
                act.copy(xA[c % XSLOTS][:, :, :].rearrange("p k n -> p (k n)"),
                         bank[chain_bank(0, c)][:, 0:D]).then_inc(xA_ready, 1)

            def down(layer, c):
                src = bank[chain_bank(layer, c)][:, D:D + P]
                if layer == 3:
                    act.wait_ge(downB_ps, c + 1)
                    if c >= XSLOTS:
                        act.wait_ge(upB_ps, c - XSLOTS + 1)
                    dst, done = hB[c % XSLOTS], hB_ready
                else:
                    i = lane_a(layer, c)
                    act.wait_ge(downA_ps, i + 1)
                    if i >= XSLOTS:
                        act.wait_ge(upA_ps, i - XSLOTS + 1)
                    dst, done = hA[i % XSLOTS], hA_ready
                if layer == 0 and c == 0:
                    act.wait_ge(chunk_vecs_ready, 1)
                act.activation(dst[:, :], src, ACT.Gelu,
                               bias=chunk_vecs[:, BD[(0, 2, 3).index(layer)], c:c + 1]).then_inc(done, 1)

            def norm0(c):
                act.wait_ge(normA_T_ps, c + 1)
                lo = act.value_load(start_tok_i[0:1, c:c + 1], min_val=0, max_val=N)
                if c == 0:
                    act.wait_ge(constants, 2)
                else:
                    act.wait_ge(x1_window, KD * c)
                for m in range(KD):
                    src = bank[chain_bank(0, c)][:, m * P:(m + 1) * P]
                    ins = act.activation(x1T[:, m, bass.ds(lo, P)], src, ACT.Identity,
                                         bias=chunk_vecs[:, BETA0 + m, c:c + 1],
                                         scale=chunk_vecs[:, GAMMA0 + m, c:c + 1])
                    ins.then_inc(x1_window, 1)

            def norm2(c):
                act.wait_ge(normA_T_ps, lane_a(2, c) + 1)
                if c >= XSLOTS:
                    act.wait_ge(downB_ps, c - XSLOTS + 1)
                for m in range(KD):
                    ins = act.activation(zB[c % XSLOTS][:, m, :], bank[chain_bank(2, c)][:, m * P:(m + 1) * P],
                                         ACT.Identity, bias=chunk_vecs[:, BETA2 + m, c:c + 1],
                                         scale=chunk_vecs[:, GAMMA2 + m, c:c + 1])
                ins.then_inc(zB_ready, 1)

            def tokens(h):
                if h:
                    act.wait_ge(mix_ps, KD * h)
                for q in range(2):
                    act.wait_ge(tokens_ps, 2 * h + q + 1)
                    act.copy(x1_tok[:, 2 * q:2 * q + 2, :].rearrange("p g n -> p (g n)"),
                             bank[2 + q][:, :]).then_inc(tokens_ready, 1)

            def project(h):
                if h:
                    act.wait_ge(scores_ps, h)
                for m in range(KD):
                    act.wait_ge(project_ps, KD * h + m + 1)
                    act.copy(y_T[:, m, :], bank[m][:, :]).then_inc(y_ready, 1)

            def scores(h):
                act.wait_ge(dots_ready, h + 1)
                act.activation(weighed[:, :, :].rearrange("p g n -> p (g n)"),
                               dots[:, :, :].rearrange("p g n -> p (g n)"), ACT.Exp, scale=SCALE).then_inc(exp_ready, 1)

            def mix(h):
                if h:
                    act.wait_ge(attend_ps, KD * h)
                for m in range(KD):
                    act.wait_ge(mix_ps, KD * h + m + 1)
                    act.copy(z[0][:, m, :], bank[m][:, :]).then_inc(z_high, 1)

            def attend(h):
                for m in range(KD):
                    act.wait_ge(attend_ps, KD * h + m + 1)
                    act.activation(ao[h][0][:, m, :], bank[m][:, :], ACT.Identity,
                                   bias=vecs[:, BP + m:BP + m + 1]).then_inc(ao_high, 1)

            def hidden(phase, j):
                n = phase * JT + j
                b = RING[n % len(RING)]
                act.wait_ge(hidden_ps, n + 1)
                bias = vecs[:, (CB1 if phase < 2 else MB1) + j:(CB1 if phase < 2 else MB1) + j + 1]
                if n >= 2:
                    act.wait_ge(g_ready, n - 1)
                act.activation(g_full[n % 2][:, :], bank[b][:, :], ACT.Gelu, bias=bias)
                if phase and j == 0:
                    act.wait_ge(outer_ps, KD * phase)
                act.activation(g[0][:, j, :], bank[b][:, :], ACT.Gelu,
                               bias=bias).then_inc(g_high, 1)

            def outer(phase, part=None):
                if phase < 2:
                    for m in range(KD):
                        act.wait_ge(cms_full_ready, KD * phase + m + 1)
                        act.copy(cms[phase][0][:, m, :], cms_full[:, m, :]).then_inc(cms_high, 1)

            do = {"vectors": vectors, "order": find_order, "fold_transpose": fold_transpose, "fold": fold,
                  "load0": load0, "down": down, "norm0": norm0, "norm2": norm2, "tokens": tokens,
                  "project": project, "scores": scores, "mix": mix, "attend": attend,
                  "hidden": hidden, "outer": outer}
            for name, *args in steps:
                if name in do:
                    do[name](*args)

        @block.vector
        def _(dve):
            own = [0]

            def link(ins):
                own[0] += 1
                ins.then_inc(dve_own, 1)
                dve.wait_ge(dve_own, own[0])

            def find_windows():
                dve.wait_ge(constants, 2)
                dve.wait_ge(ids_in, 48)
                link(dve.tensor_scalar(past[:, :], seq_from[:, :], part_col[:, 0:1], None, ALU.is_le))
                link(dve.tensor_reduce(seq_col[:, :], past[:, :], X_AXIS, ALU.add))
                dve.tensor_scalar(tok_spare[:, :], seq_col[:, :], -float(S), -float(N), ALU.mult, ALU.add)
                dve.tensor_copy(key_col[:, 1:2], role_col_i[:, 1:2])
                link(dve.tensor_scalar(roles[:, :], roles_i[:, :], 0.0, float(R - 1), ALU.max, ALU.min))
                link(dve.tensor_scalar(key_col[:, 0:1], role_col_i[:, 0:1], 0.0, float(R - 1), ALU.max, ALU.min))
                link(dve.tensor_scalar(key_col[:, 0:1], key_col[:, 0:1], float(B), part_col[0:B, :], ALU.mult, ALU.add))
                link(dve.scalar_tensor_tensor(out=keys[:, :], in0=roles[:, :], scalar=float(B),
                                              in1=pos_row[:, 0:B], op0=ALU.mult, op1=ALU.add))
                link(dve.tensor_scalar(below[:, :], keys[0:B, :], key_col[:, 0:1], None, ALU.is_lt))
                link(dve.tensor_reduce(pos_col[:, :], below[:, :], X_AXIS, ALU.add))
                dve.tensor_scalar(sorts[:, :], pos_row[0:B, :], pos_col[:, 0:1], None, ALU.is_equal)
                dve.tensor_copy(spread[:, 0, :], part_col[0:B, :].to_broadcast([B, P]))
                dve.tensor_copy(spread[:, 1, :], key_col[:, 1:2].to_broadcast([B, P])).then_inc(sorts_ready, 1)
                link(dve.tensor_tensor(is_role[:, :, :], roles[:, :].unsqueeze(1).to_broadcast([P, R, B]),
                                       role_row[:, :, :], ALU.is_equal))
                link(dve.tensor_reduce(count[:, :], is_role[:, :, :], X_AXIS, ALU.add))
                link(dve.tensor_tensor(more[:, :, :], count[:, :].unsqueeze(2).to_broadcast([P, R, 8]),
                                       four_row[:, :, :], ALU.is_gt))
                link(dve.tensor_reduce(wins[:, :], more[:, :, :], X_AXIS, ALU.add))
                dve.tensor_scalar(ends4[:, 0:1], wins[:, 0:1], float(WB), None, ALU.mult)
                dve.scalar_tensor_tensor(out=short[:, :], in0=wins[:, 0:2], scalar=-float(WB),
                                         in1=count[:, 0:2], op0=ALU.mult, op1=ALU.add)
                link(dve.tensor_scalar(ends4[:, 1:2], wins[:, 1:2], wins[:, 0:1], float(WB), ALU.add, ALU.mult))
                link(dve.tensor_tensor(later[:, :, :], chunk4_row[:, :].unsqueeze(1).to_broadcast([P, 2, CHUNKS]),
                                       ends4[:, :].unsqueeze(2).to_broadcast([P, 2, CHUNKS]), ALU.is_ge))
                link(dve.tensor_tensor(chunk_role[:, :], later[:, 0, :], later[:, 1, :], ALU.add))
                dve.tensor_copy(chunk_role_i[:, :], chunk_role[:, :])
                dve.tensor_scalar(end[:, :], later[:, 0, :], count[:, 1:2], count[:, 0:1], ALU.mult, ALU.add)
                link(dve.scalar_tensor_tensor(out=start[:, :], in0=later[:, 0, :], scalar=short[:, 0:1],
                                              in1=chunk4_row[:, :], op0=ALU.mult, op1=ALU.add))
                link(dve.scalar_tensor_tensor(out=start[:, :], in0=later[:, 1, :], scalar=short[:, 1:2],
                                              in1=start[:, :], op0=ALU.mult, op1=ALU.add))
                link(dve.tensor_scalar(start[:, :], start[:, :], float(B), None, ALU.min))
                dve.tensor_scalar(start_tok_i[:, :], start[:, :], float(S), None, ALU.mult).then_inc(chunks_ready, 1)
                link(dve.scalar_tensor_tensor(out=end[:, :], in0=later[:, 1, :], scalar=count[:, 2:3],
                                              in1=end[:, :], op0=ALU.mult, op1=ALU.add))
                link(dve.tensor_tensor(reach[:, :, :], pos_row[:, :].unsqueeze(1).to_broadcast([P, CHUNKS, POS]),
                                       start[:, :].unsqueeze(2).to_broadcast([P, CHUNKS, POS]), ALU.subtract))

            def find_order():
                dve.wait_ge(order_ready, 1)
                link(dve.scalar_tensor_tensor(out=reach[:, :, :], in0=reach[:, :, :], scalar=seq_col[:, 0:1],
                                              in1=order[:, 0, :].unsqueeze(1).to_broadcast([P, CHUNKS, POS]),
                                              op0=ALU.is_equal, op1=ALU.mult))
                link(dve.tensor_reduce(seq_at[:, :], reach[:, :, :], X_AXIS, ALU.add))
                dve.tensor_copy(seq_at_i[:, :], seq_at[:, :]).then_inc(seqs_ready, 1)
                dve.scalar_tensor_tensor(out=valid[:, :], in0=start[:, :], scalar=seq_col[:, 0:1], in1=end[:, :],
                                         op0=ALU.add, op1=ALU.is_lt)
                link(dve.tensor_scalar(row_at[:, :], seq_at[:, :], float(S), tok_spare[:, 0:1], ALU.mult, ALU.add))
                link(dve.tensor_tensor(row_at[:, :], row_at[:, :], valid[:, :], ALU.mult))
                dve.tensor_scalar(row_at_i[:, :], row_at[:, :], spare_col[:, 0:1], None, ALU.add).then_inc(rows_ready, 1)

            def vectors():
                dve.wait_ge(vectors_ready, 1)
                link(dve.tensor_tensor(role_hot[:, :, :], chunk_role[:, :].unsqueeze(2).to_broadcast([P, CHUNKS, R]),
                                       role_in[:, :, :], ALU.is_equal))
                for v in range(PER_ROLE):
                    ins = dve.tensor_tensor(picked[:, v, :, :], role_hot[:, :, :],
                                            vecs[:, R * v:R * (v + 1)].unsqueeze(1).to_broadcast([P, CHUNKS, R]),
                                            ALU.mult)
                link(ins)
                dve.tensor_reduce(chunk_vecs[:, :, :], picked[:, :, :, :], X_AXIS, ALU.add).then_inc(chunk_vecs_ready, 1)
                for m in range(KD):
                    ins = dve.tensor_scalar(target[:, m, :], order[:, 1, :], (part_col, part_col2)[m][:, 0:1],
                                            vecs[:, CB2 + m:CB2 + m + 1], ALU.is_equal, ALU.add)
                ins.then_inc(target_ready, 1)

            def fold():
                for n, w in enumerate((wqk, wvp)):
                    dve.wait_ge(fold_high, n + 1)
                    dve.tensor_tensor(w[1][:, :, :].rearrange("p k n -> p (k n)"), bank[5 + n][:, :],
                                      w[0][:, :, :].rearrange("p k n -> p (k n)").bitcast(F32),
                                      ALU.subtract).then_inc(fold_ready, 1)

            def weights(p):
                slot, fill = filling(p)
                _, view, parts = pieces[p]
                if p == 4:
                    dve.wait_ge(attend_ps, 2 * KD)
                    dve.wait_ge(beta_ready, 1)
                if p == 8:
                    dve.wait_ge(hidden_ps, 2 * JT)
                dve.wait_ge(stage_in[slot], 16 * fill + (16 if slot < 2 else 0))
                dve.tensor_copy(parts[0], view(slot)).then_inc(w_high, 1)

            def moments(y, st, mv, var, k, bank_ap, done, summed, n):
                dve.tensor_tensor(y, bank_ap, y, ALU.add).then_inc(summed, 1)
                dve.wait_ge(summed, n + 1)
                link(dve.bn_stats(st[:, k, :], y))
                link(dve.bn_aggr(mv[:, k, :], st[:, k, :]))
                dve.tensor_scalar(var[:, k, 0:1], mv[:, k, 1:2], LN_EPS, None, ALU.add).then_inc(done, 1)

            def load2(c):
                i = lane_a(2, c)
                dve.wait_ge(x2_ready, KD if c < 4 else 2 * KD)
                dve.wait_ge(downA_ps, i - XSLOTS + 1)
                if c == 0:
                    dve.wait_ge(tables_in, 6 * 16)
                lo = dve.value_load(start_tok_i[0:1, c:c + 1], min_val=0, max_val=N)
                dve.tensor_copy(xA[i % XSLOTS][:, :, :], x1T[:, :, bass.ds(lo, P)]).then_inc(xA_ready, 1)
                r = dve.value_load(chunk_role_i[0:1, c:c + 1], min_val=0, max_val=R - 1)
                dve.wait_ge(xT_ps, i + 1)
                dve.wait_ge(normA_T_ps, i - YSLOTS + 1)
                if c >= YSLOTS:
                    dve.wait_ge(resB_half, c - YSLOTS + 1)
                dve.tensor_tensor(yA[i % YSLOTS][:, :], bank[chain_bank(2, c)][:, 0:D],
                                  table["bu2"][:, bass.ds(r, 1), :].rearrange("p r n -> p (r n)"),
                                  ALU.add).then_inc(resA_ready, 1)

            def up(layer, c):
                if layer == 3:
                    k = c % YSLOTS
                    dve.wait_ge(upB_ps, c + 1)
                    dve.wait_ge(resB_ready, c + 1)
                    moments(yB[k][:, :], statsB, mvB, rstdB, k, bank[chain_bank(3, c)][:, 0:D], varB_ready,
                            sumB_ready, c)
                else:
                    i = lane_a(layer, c)
                    k = i % YSLOTS
                    dve.wait_ge(upA_ps, i + 1)
                    dve.wait_ge(resA_ready, i + 1)
                    moments(yA[k][:, :], statsA, mvA, rstdA, k, bank[chain_bank(layer, c)][:, 0:D], varA_ready,
                            sumA_ready, i)

            def norm(layer, c):
                i = lane_a(layer, c)
                k = i % YSLOTS
                dve.wait_ge(rstdA_ready, i + 1)
                dve.tensor_scalar(yA[k][:, :], yA[k][:, :], mvA[:, k, 0:1], rstdA[:, k, 1:2],
                                  ALU.subtract, ALU.mult).then_inc(normA_ready, 1)

            def norm3(c):
                k = c % YSLOTS
                r = dve.value_load(chunk_role_i[0:1, c:c + 1], min_val=0, max_val=R - 1)
                dve.wait_ge(rstdB_ready, c + 1)
                link(dve.scalar_tensor_tensor(out=yB[k][:, :], in0=yB[k][:, :], scalar=mvB[:, k, 0:1],
                                              in1=table["gamma3"][:, bass.ds(r, 1), :].rearrange("p r n -> p (r n)"),
                                              op0=ALU.subtract, op1=ALU.mult))
                dve.scalar_tensor_tensor(out=yB[k][:, :], in0=yB[k][:, :], scalar=rstdB[:, k, 1:2],
                                         in1=table["beta3"][:, bass.ds(r, 1), :].rearrange("p r n -> p (r n)"),
                                         op0=ALU.mult, op1=ALU.add).then_inc(out_ready, 1)

            def project(h):
                dve.wait_ge(x1_window, KD * (6 if h == 0 else CHUNKS))
                if h:
                    dve.wait_ge(project_ps, KD * h)
                src = x1T[:, :, h * HALF:(h + 1) * HALF]
                link(dve.tensor_copy(x1[0][:, :, :], src))
                dve.tensor_tensor(x1[1][:, :, :], src, x1[0][:, :, :].bitcast(F32), ALU.subtract).then_inc(x1_split, 1)

            def scores(h):
                dve.wait_ge(scores_ps, h + 1)
                for q in range(WB):
                    lo, hi = S * q, S * (q + 1)
                    src = bank[2][lo:hi, :].rearrange("p (g n) -> p g n", n=P)
                    ins = dve.tensor_copy(dots[lo:hi, :, :], src[:, :, lo:hi])
                ins.then_inc(dots_copied, 1)
                dve.wait_ge(dots_copied, h + 1)
                link(dve.tensor_reduce(peak[:, :], dots[:, :, :], X_AXIS, ALU.max))
                dve.tensor_tensor(dots[:, :, :], dots[:, :, :], peak[:, :].unsqueeze(2).to_broadcast([P, G, S]),
                                  ALU.subtract).then_inc(dots_ready, 1)

            def mix(h):
                dve.wait_ge(exp_ready, h + 1)
                link(dve.tensor_reduce(total[:, :], weighed[:, :, :], X_AXIS, ALU.add))
                link(dve.reciprocal(inv_total[:, :], total[:, :]))
                link(dve.tensor_tensor(probs[:, :, :], weighed[:, :, :],
                                       inv_total[:, :].unsqueeze(2).to_broadcast([P, G, S]), ALU.mult))
                if h:
                    dve.wait_ge(mix_ps, KD * h)
                for q in range(WB):
                    lo, hi = S * q, S * (q + 1)
                    ins = dve.transpose(probs_T[lo:hi, :, lo:hi], probs[lo:hi, :, :])
                ins.then_inc(probs_ready, 1)
                for m in range(KD):
                    dve.wait_ge(z_high, KD * h + m + 1)
                    dve.tensor_tensor(z[1][:, m, :], bank[m][:, :], z[0][:, m, :].bitcast(F32),
                                      ALU.subtract).then_inc(z_ready, 1)

            def attend(h):
                for m in range(KD):
                    dve.wait_ge(ao_high, KD * h + m + 1)
                    dve.scalar_tensor_tensor(out=ao[h][1][:, m, :], in0=bank[m][:, :],
                                             scalar=vecs[:, BP + m:BP + m + 1], in1=ao[h][0][:, m, :].bitcast(F32),
                                             op0=ALU.add, op1=ALU.subtract).then_inc(ao_ready, 1)

            def hidden(phase, j):
                n = phase * JT + j
                dve.wait_ge(g_high, n + 1)
                dve.tensor_tensor(g[1][:, j, :], g_full[n % 2][:, :], g[0][:, j, :].bitcast(F32),
                                  ALU.subtract).then_inc(g_ready, 1)

            def outer(phase, part=None):
                if part not in (None, 3):
                    return
                h = phase % 2
                if phase < 2:
                    if phase == 0:
                        dve.wait_ge(target_ready, 1)
                    else:
                        dve.wait_ge(sum_ready, KD)
                    for m in range(KD):
                        dve.wait_ge(outer_ps, KD * phase + m + 1)
                        dve.tensor_tensor(cms_full[:, m, :].rearrange("p (b s) -> p b s", s=S),
                                          bank[m][:, :].rearrange("p (b s) -> p b s", s=S),
                                          target[:, m, h * (B // 2):(h + 1) * (B // 2)].unsqueeze(2).to_broadcast([P, B // 2, S]),
                                          ALU.add).then_inc(cms_full_ready, 1)
                    for m in range(KD):
                        dve.wait_ge(cms_high, KD * phase + m + 1)
                        dve.tensor_tensor(cms[h][1][:, m, :], cms_full[:, m, :], cms[h][0][:, m, :].bitcast(F32),
                                          ALU.subtract).then_inc(cms_ready, 1)
                else:
                    dve.wait_ge(sum_ready, KD * (h + 1))
                    for m in range(KD):
                        dve.wait_ge(outer_ps, KD * phase + m + 1)
                        half = x1T[:, m, h * HALF:(h + 1) * HALF]
                        ins = dve.scalar_tensor_tensor(out=half, in0=bank[m][:, :], scalar=vecs[:, MB2 + m:MB2 + m + 1],
                                                       in1=half, op0=ALU.add, op1=ALU.add)
                        ins.then_inc(x2_sum, 1)
                        dve.wait_ge(x2_sum, KD * h + m + 1)
                        dve.tensor_scalar(half, half, 0.0, 1.0, ALU.max, ALU.min).then_inc(x2_ready, 1)

            find_windows()
            do = {"vectors": lambda: None, "order": lambda: (find_order(), vectors()), "fold": fold,
                  "weights": weights, "load2": load2, "up": up,
                  "norm0": lambda c: norm(0, c), "norm2": lambda c: norm(2, c), "norm3": norm3,
                  "project": project, "scores": scores, "mix": mix, "attend": attend,
                  "hidden": hidden, "outer": outer}
            for name, *args in steps:
                if name in do:
                    do[name](*args)

        @block.gpsimd
        def _(pool):
            own = [0]

            def link(ins):
                own[0] += 1
                ins.then_inc(pool_own, 1)
                pool.wait_ge(pool_own, own[0])

            link(pool.memset(ident[:, :], 0.0))
            pool.affine_select(out=ident[:, :], in_=ident[:, :], compare_op=ALU.not_equal, fill=1.0, base=0,
                               pattern=[[-1, P]], channel_multiplier=1).then_inc(constants, 1)

            def iota(dst, pattern, base=0, mult=0):
                return pool.iota(dst, pattern, base=base, channel_multiplier=mult,
                                 allow_small_or_imprecise_dtypes=True)

            iota(pos_row[:, :], [[1, POS]])
            iota(part_col[:, :], [[0, 1]], 0, 1)
            iota(role_row[:, :, :], [[1, R], [0, B]])
            iota(four_row[:, :, :], [[0, R], [WB, 8]])
            iota(chunk4_row[:, :], [[WB, CHUNKS]])
            iota(role_in[:, :, :], [[0, CHUNKS], [1, R]])
            iota(part_col2[:, :], [[0, 1]], P, 1)
            iota(spare_col[:, :], [[0, 1]], N, 1)
            iota(seq_from[:, :], [[S, WB - 1]], S, 0)
            pool.memset(power[:, :], -0.5)
            pool.memset(x1T[:, :, N:POS * S], 0.0)
            pool.memset(probs_T[:, :, :], 0.0).then_inc(constants, 1)

            def weights(p):
                slot, _ = filling(p)
                _, view, parts = pieces[p]
                pool.wait_ge(w_high, p + 1)
                pool.tensor_tensor(parts[1], view(slot), parts[0].bitcast(F32), ALU.subtract).then_inc(w_ready, 1)

            def load0(c):
                if c == 0:
                    pool.wait_ge(table0_in, 16)
                    pool.wait_ge(chunks_ready, 1)
                r = pool.value_load(chunk_role_i[0:1, c:c + 1], min_val=0, max_val=R - 1)
                pool.wait_ge(x_in[c % 4], 16 * WB * (c // 4 + 1))
                if c >= YSLOTS:
                    pool.wait_ge(normA_T_ps, c - YSLOTS + 1)
                pool.tensor_tensor(yA[c % YSLOTS][:, :], x_tok[c % 4][:, :],
                                   table["bu0"][:, bass.ds(r, 1), :].rearrange("p r n -> p (r n)"),
                                   ALU.add).then_inc(resA_ready, 1)

            def up(layer, c):
                if layer == 3:
                    pool.wait_ge(varB_ready, c + 1)
                    k = c % YSLOTS
                    pool.tensor_tensor(rstdB[:, k, 1:2], rstdB[:, k, 0:1], power[:, :], ALU.pow).then_inc(rstdB_ready, 1)
                else:
                    i = lane_a(layer, c)
                    pool.wait_ge(varA_ready, i + 1)
                    k = i % YSLOTS
                    pool.tensor_tensor(rstdA[:, k, 1:2], rstdA[:, k, 0:1], power[:, :], ALU.pow).then_inc(rstdA_ready, 1)

            def norm2(c):
                i = lane_a(2, c)
                r = pool.value_load(chunk_role_i[0:1, c:c + 1], min_val=0, max_val=R - 1)
                pool.wait_ge(normA_ready, i + 1)
                if c >= YSLOTS:
                    pool.wait_ge(out_done[c % YSLOTS], 16 * (c // YSLOTS))
                pool.tensor_tensor(yB[c % YSLOTS][:, :], yA[i % YSLOTS][:, :],
                                   table["gamma2"][:, bass.ds(r, 1), :].rearrange("p r n -> p (r n)"),
                                   ALU.mult).then_inc(resB_half, 1)
                pool.wait_ge(resB_half, c + 1)
                pool.tensor_tensor(yB[c % YSLOTS][:, :], yB[c % YSLOTS][:, :],
                                   table["beta2"][:, bass.ds(r, 1), :].rearrange("p r n -> p (r n)"),
                                   ALU.add).then_inc(resB_ready, 1)

            def norm3(c):
                if c == 0:
                    pool.wait_ge(rows_ready, 1)
                pool.wait_ge(out_ready, c + 1)
                pool.indirect_dma_start(
                    out=out.rearrange("b s d -> (b s) d"),
                    out_offset=bass.IndirectOffsetOnAxis(ap=row_at_i[:, c:c + 1], axis=0),
                    in_=yB[c % YSLOTS][:, :], in_offset=None,
                    bounds_check=N - 1, oob_is_err=False).then_inc(out_done[c % YSLOTS], 16)

            def outer(phase, part=None):
                if phase < 2:
                    for m in range(KD):
                        pool.wait_ge(cms_full_ready, KD * phase + m + 1)
                        half = x1T[:, m, phase * HALF:(phase + 1) * HALF]
                        pool.tensor_tensor(half, half, cms_full[:, m, :], ALU.add).then_inc(sum_ready, 1)

            def tables():
                pool.wait_ge(tables_in, 6 * 16)
                pool.tensor_tensor(table["beta2"][:, :, :], table["beta2"][:, :, :], table["bu3"][:, :, :],
                                   ALU.add).then_inc(beta_ready, 1)

            do = {"tables": tables, "weights": weights, "load0": load0, "up": up, "norm2": norm2, "norm3": norm3, "outer": outer}
            for name, *args in steps:
                if name in do:
                    do[name](*args)
            for k in range(YSLOTS):
                pool.wait_ge(out_done[k], 16 * len(range(k, CHUNKS, YSLOTS)))


def kernel(**inputs):
    import numpy as np
    import concourse.bacc as bacc
    from concourse.bass_utils import run_bass_kernel_spmd

    nc = bacc.Bacc("TRN2", target_bir_lowering=False, num_devices=1)
    arrays, aps = {}, {}
    for name, value in inputs.items():
        if name == "_lenS":
            continue
        v = np.ascontiguousarray(value)
        arrays[f"in_{name}"] = v
        aps[name] = nc.dram_tensor(f"in_{name}", v.shape, mybir.dt.from_np(v.dtype), kind="ExternalInput").ap()
    out = nc.dram_tensor("out", (B, S, D), F32, kind="ExternalOutput").ap()
    build(nc, aps, out)
    return run_bass_kernel_spmd(nc, [arrays], core_ids=[0]).results[0]["out"]
```

```python
from contextlib import ExitStack

import concourse.bass as bass
from concourse import mybir

F32 = mybir.dt.float32
F32R = mybir.dt.float32r
I32 = mybir.dt.int32
U32 = mybir.dt.uint32
ALU = mybir.AluOpType
ACT = mybir.ActivationFunctionType
X_AXIS = mybir.AxisListType.X

P = 128
B, S, D = 32, 32, 256
N = B * S
R = 3
KD = D // P
HID = 4 * D
JT = HID // P
HALF = N // 2
G = HALF // P
WB = P // S
CHUNKS = (B + R * (WB - 1)) // WB
POS = B + WB
LN_EPS = 1e-5
SCALE = float(D) ** -0.5

BD, GAMMA0, BETA0, GAMMA2, BETA2 = (0, 1, 2), 3, 5, 7, 9
PER_ROLE = 11
BP = PER_ROLE * R
CB1, CB2 = BP + KD, BP + KD + JT
MB1, MB2 = CB2 + KD, CB2 + KD + JT
ROWS = MB2 + KD

XSLOTS, YSLOTS, WSLOTS, TSLOTS = 3, 4, 4, 6
PHASES = ((0, HALF), (HALF, HALF), (0, HALF), (HALF, HALF // 2), (HALF + HALF // 2, HALF // 2))
DVE_PIECES = 2
STAGE = 3


def plan():
    steps = [("fold_transpose", 0), ("order",), ("fold_transpose", 1), ("fold", 0), ("vectors",)]

    def ticks(stages, t, lo, hi):
        for name, late in stages:
            c = lo + t - late
            if lo <= c < hi:
                steps.append((name[:-1], int(name[-1]), c))

    first = (("center0", 3), ("up0", 2), ("down0", 1), ("turn0", 4), ("load0", 0))
    last = (("center2", 2), ("up2", 1), ("turn2", 3), ("down2", 0), ("load2", -1), ("up3", 5), ("finish3", 6), ("down3", 4))

    def tick0(t):
        ticks(first, t, 0, CHUNKS)

    for t in range(10):
        tick0(t)
        if t in (2, 5):
            steps.append(("weights", (2, 5).index(t)))
        if t == 3:
            steps.append(("fold", 1))
    steps.extend([("tokens", 0), ("project", 0)])
    tick0(10)
    steps.extend([("scores", 0)])
    tick0(11)
    tick0(12)
    steps.extend([("mix", 0), ("weights", 2)])
    tick0(13)
    steps.extend([("attend", 0), ("tokens", 1), ("project", 1), ("weights", 3)])
    steps.extend([("hidden", 0, j) for j in range(2)])
    steps.extend([("scores", 1)])
    steps.extend([("hidden", 0, j) for j in range(2, 5)])
    steps.extend([("mix", 1)])
    steps.extend([("hidden", 0, j) for j in range(5, 6)])
    steps.extend([("attend", 1)])
    steps.extend([("hidden", 0, j) for j in range(6, 8)])
    steps.extend([("weights", 4), ("outer", 0, 0), ("weights", 5)])
    for j in range(JT):
        steps.append(("hidden", 1, j))
        if j in (1, 4):
            steps.append(("weights", 6 + (j == 4)))
    steps.extend([("outer", 1, 0), ("weights", 8)])
    for j in range(JT):
        steps.append(("hidden", 2, j))
        if j == 3:
            steps.append(("weights", 9))
    steps.extend([("outer", 2, 0)])

    def with_chain(phase, lo, hi):
        units = [("hidden", phase, j) for j in range(JT)] + [("outer", phase, q) for q in range(4)]
        count = hi - lo + 7
        done = 0
        for n, unit in enumerate(units):
            steps.append(unit)
            while done * len(units) < (n + 1) * count:
                ticks(last, done - 1, lo, hi)
                done += 1

    with_chain(3, 0, 4)
    with_chain(4, 4, 6)
    for t in range(-1, CHUNKS - 6 + 6):
        ticks(last, t, 6, CHUNKS)
    return steps


def build(nc, a, out):
    steps = plan()
    with ExitStack() as ctx:
        at = [(nc.sbuf_base + 31) // 32 * 32]

        def place(name, shape, dt, offset=None):
            size = 4
            for n in shape[1:]:
                size *= n
            size = (size + 31) // 32 * 32
            if offset is None:
                offset = at[0]
                at[0] += size
            return nc.alloc_sbuf_tensor_at(name, shape, dt, offset=offset)

        def sem(name):
            return ctx.enter_context(nc.semaphore(name))

        bank = [ctx.enter_context(nc.psum_tensor(f"bank{b}", [P, 512], F32)) for b in range(8)]

        ident = place("ident", [P, P], F32)
        pos_row = place("pos_row", [P, POS], F32)
        chunk4_row = place("chunk4_row", [P, CHUNKS], F32)
        role_row = place("role_row", [P, R, B], F32)
        four_row = place("four_row", [P, R, 8], F32)
        tok_col = place("tok_col", [P, 1], F32)
        role_in = place("role_in", [P, CHUNKS, R], F32)
        part_col = place("part_col", [P, 1], F32)
        part_col2 = place("part_col2", [P, 1], F32)
        seq_col = place("seq_col", [P, 1], F32)
        seq_from = place("seq_from", [P, WB - 1], F32)
        past = place("past", [P, WB - 1], F32)
        spare_col = place("spare_col", [P, 1], F32)
        tok_spare = place("tok_spare", [P, 1], F32)
        power = place("power", [P, 1], F32)
        roles_i = place("roles_i", [P, B], I32)
        role_col_i = place("role_col_i", [B, 2], I32)
        roles = place("roles", [P, B], F32)
        keys = place("keys", [P, B], F32)
        key_col = place("key_col", [B, 1], F32)
        below = place("below", [B, B], F32)
        pos_col = place("pos_col", [B, 1], F32)
        sorts = place("sorts", [B, POS], F32)
        spread = place("spread", [B, 2, P], F32)
        is_role = place("is_role", [P, R, B], F32)
        count = place("count", [P, R], F32)
        more = place("more", [P, R, 8], F32)
        wins = place("wins", [P, R], F32)
        ends4 = place("ends4", [P, 2], F32)
        short = place("short", [P, 2], F32)
        later = place("later", [P, 2, CHUNKS], F32)
        chunk_role = place("chunk_role", [P, CHUNKS], F32)
        start = place("start", [P, CHUNKS], F32)
        end = place("end", [P, CHUNKS], F32)
        start_tok_i = place("start_tok_i", [P, CHUNKS], I32)
        chunk_role_i = place("chunk_role_i", [P, CHUNKS], I32)
        order = place("order", [P, 2, POS], F32)
        reach = place("reach", [P, CHUNKS, POS], F32)
        seq_at = place("seq_at", [P, CHUNKS], F32)
        from_row_i = place("from_row_i", [P, CHUNKS], U32)
        valid = place("valid", [P, CHUNKS], F32)
        row_at = place("row_at", [P, CHUNKS], F32)
        row_at_i = place("row_at_i", [P, CHUNKS], U32)
        role_hot = place("role_hot", [P, CHUNKS, R], F32)
        vec_rows = place("vec_rows", [ROWS, P], F32)
        vecs = place("vecs", [P, ROWS], F32)
        picked = place("picked", [P, PER_ROLE, CHUNKS, R], F32)
        chunk_vecs = place("chunk_vecs", [P, PER_ROLE, CHUNKS], F32)
        target = place("target", [P, KD, POS], F32)

        stage = [place(f"stage{i}", [P, HID], F32) for i in range(STAGE)]
        wdA = [place(f"wdA{i}", [P, KD, P], F32) for i in range(WSLOTS)]
        wuA = [place(f"wuA{i}", [P, D], F32) for i in range(WSLOTS)]
        wdB = [place(f"wdB{i}", [P, KD, P], F32) for i in range(WSLOTS)]
        wuB = [place(f"wuB{i}", [P, D], F32) for i in range(WSLOTS)]
        xA = [place(f"xA{i}", [P, KD, P], F32) for i in range(XSLOTS)]
        hA = [place(f"hA{i}", [P, P], F32) for i in range(XSLOTS)]
        yA = [place(f"yA{i}", [P, D], F32) for i in range(YSLOTS)]
        zB = [place(f"zB{i}", [P, KD, P], F32) for i in range(XSLOTS)]
        hB = [place(f"hB{i}", [P, P], F32) for i in range(XSLOTS)]
        yB = [place(f"yB{i}", [P, D], F32) for i in range(YSLOTS)]
        statsA = place("statsA", [P, YSLOTS, 6], F32)
        mvA = place("mvA", [P, YSLOTS, 2], F32)
        rstdA = place("rstdA", [P, YSLOTS, 2], F32)
        statsB = place("statsB", [P, YSLOTS, 6], F32)
        mvB = place("mvB", [P, YSLOTS, 2], F32)
        rstdB = place("rstdB", [P, YSLOTS, 2], F32)
        table = {}
        for name in ("gamma3", "beta3"):
            table[name] = place(f"table_{name}", [P, R, D], F32)
        bu_rows = place("bu_rows", [P, D], F32)
        bu = [place(f"bu_{x}", [P, D], F32R) for x in "hl"]
        hot_col = place("hot_col", [P, CHUNKS], F32)
        hot = place("hot", [P, CHUNKS, P], F32R)
        x1T = place("x1T", [P, KD, POS * S], F32)
        cw1_at = at[0]
        cw1 = [place(f"cw1_{x}", [P, KD, HID], F32R) for x in "hl"]
        cw2_at = at[0]
        cw2 = [place(f"cw2_{x}", [P, JT, D], F32R) for x in "hl"]
        mw2 = [place(f"mw2_{x}", [P, JT, D], F32R, cw1_at + n * 4 * JT * D) for n, x in enumerate("hl")]
        ao = [[place(f"ao{h}_{x}", [P, KD, HALF], F32R) for x in "hl"] for h in range(2)]
        g = [place(f"g_{x}", [P, JT, HALF], F32R) for x in "hl"]
        g_full = [place(f"g_full{i}", [P, HALF], F32) for i in range(2)]

        early = at[0]
        x_tok = [place(f"x_tok{i}", [P, D], F32) for i in range(TSLOTS)]
        y_T = place("y_T", [P, KD, HALF], F32, at[0])
        wT = {w: place(f"wT_{w}", [P, KD, D], F32) for w in "qkv"}
        wqk = [place(f"wqk_{x}", [P, KD, D], F32R) for x in "hl"]
        wvp = [place(f"wvp_{x}", [P, KD, D], F32R) for x in "hl"]
        x1 = [place(f"x1_{x}", [P, KD, HALF], F32R) for x in "hl"]
        x1_tok = place("x1_tok", [P, G, D], F32)
        probs_T = place("probs_T", [P, G, P], F32)
        dots = place("dots", [P, G, S], F32)
        weighed = place("weighed", [P, G, S], F32)
        probs = place("probs", [P, G, S], F32)
        peak = place("peak", [P, G], F32)
        total = place("total", [P, G], F32)
        inv_total = place("inv_total", [P, G], F32)
        z = [place(f"z_{x}", [P, KD, HALF], F32R) for x in "hl"]
        early_end = at[0]

        at[0] = early
        mw1 = [place(f"mw1_{x}", [P, 2 * KD, HID], F32R) for x in "hl"]
        cms = [[place(f"cms0_{x}", [P, KD, HALF], F32R) for x in "hl"],
               [place(f"cms1_{x}", [P, KD, HALF], F32R, cw2_at + n * 4 * KD * HALF) for n, x in enumerate("hl")]]
        cms_full = place("cms_full", [P, KD, HALF], F32)
        at[0] = max(at[0], early_end)

        ids_in = sem("ids_in")
        vectors_in = sem("vectors_in")
        tables_in = sem("tables_in")
        stage_in = [sem(f"stage_in{i}") for i in range(STAGE)]
        wA_in = [sem(f"wA_in{i}") for i in range(WSLOTS)]
        wB_in = [sem(f"wB_in{i}") for i in range(WSLOTS)]
        x_in = [sem(f"x_in{i}") for i in range(TSLOTS)]
        bu_in = sem("bu_in")
        bu_high = sem("bu_high")
        bu_ready = sem("bu_ready")
        hot_col_ready = sem("hot_col_ready")
        hot_ready = sem("hot_ready")
        out_done = [sem(f"out_done{i}") for i in range(YSLOTS)]
        constants = sem("constants")
        dve_own = sem("dve_own")
        pool_own = sem("pool_own")
        sorts_ready = sem("sorts_ready")
        spread_ready = sem("spread_ready")
        order_ps = sem("order_ps")
        chunks_ready = sem("chunks_ready")
        rows_in_ready = sem("rows_in_ready")
        rows_ready = sem("rows_ready")
        vectors_ps = sem("vectors_ps")
        vectors_ready = sem("vectors_ready")
        chunk_vecs_ready = sem("chunk_vecs_ready")
        target_ready = sem("target_ready")
        wT_ps = sem("wT_ps")
        wT_ready = sem("wT_ready")
        fold_ps = sem("fold_ps")
        fold_high = sem("fold_high")
        fold_ready = sem("fold_ready")
        w_high = sem("w_high")
        w_ready = sem("w_ready")
        order_ready = sem("order_ready")
        sumA_ready = sem("sumA_ready")
        sumB_ready = sem("sumB_ready")
        dots_copied = sem("dots_copied")
        x2_sum = sem("x2_sum")
        xT_ps = sem("xT_ps")
        resA_ready = sem("resA_ready")
        resB_ready = sem("resB_ready")
        xA_ready = sem("xA_ready")
        downA_ps = sem("downA_ps")
        hA_ready = sem("hA_ready")
        upA_ps = sem("upA_ps")
        varA_ready = sem("varA_ready")
        rstdA_ready = sem("rstdA_ready")
        normA_ready = sem("normA_ready")
        normA_T_ps = sem("normA_T_ps")
        x1_window = sem("x1_window")
        zB_ready = sem("zB_ready")
        downB_ps = sem("downB_ps")
        hB_ready = sem("hB_ready")
        upB_ps = sem("upB_ps")
        varB_ready = sem("varB_ready")
        rstdB_ready = sem("rstdB_ready")
        out_ready = sem("out_ready")
        tokens_ps = sem("tokens_ps")
        tokens_ready = sem("tokens_ready")
        x1_split = sem("x1_split")
        project_ps = sem("project_ps")
        y_ready = sem("y_ready")
        scores_ps = sem("scores_ps")
        dots_ready = sem("dots_ready")
        exp_ready = sem("exp_ready")
        probs_ready = sem("probs_ready")
        mix_ps = sem("mix_ps")
        z_high = sem("z_high")
        z_ready = sem("z_ready")
        attend_ps = sem("attend_ps")
        ao_high = sem("ao_high")
        ao_ready = sem("ao_ready")
        hidden_ps = sem("hidden_ps")
        g_high = sem("g_high")
        g_ready = sem("g_ready")
        outer_ps = sem("outer_ps")
        cms_full_ready = sem("cms_full_ready")
        cms_high = sem("cms_high")
        cms_ready = sem("cms_ready")
        sum_ready = sem("sum_ready")
        x2_ready = sem("x2_ready")

        def lane_a(layer, c):
            return c if layer == 0 else CHUNKS + c

        def chain_bank(layer, c):
            if layer == 0:
                return 4 + c % 3
            if layer == 2:
                return 4 + c % 2
            return 6 if c < 6 or c % 2 else 3

        def turn_bank(layer, c):
            return 7 if layer == 0 or c < 6 or c % 2 else 2

        def ring_bank(phase, j):
            return 2 + j % (3 if phase < 3 else 2)

        def first_final(c):
            return 1 + sum(WB * (c + 1) * S > tok for tok, _ in PHASES[3:])

        def half_of(phase):
            lo, width = PHASES[phase]
            return lo // HALF, slice(lo % HALF, lo % HALF + width)

        def rows(w, t):
            return a[w][t * P:(t + 1) * P, :]

        def four_tiles(w, t):
            return a[w][t * 4 * P:(t + 1) * 4 * P, :].rearrange("(k p) n -> p k n", p=P)

        def wide(slot):
            return stage[slot][:, :]

        def tiled(slot):
            return stage[slot][:, :].rearrange("p (k n) -> p k n", n=D)

        pieces = []
        for t in range(KD):
            pieces.append((rows("L1_cond_cW1", t), wide, [w[:, t, :] for w in cw1]))
        for t in range(2):
            pieces.append((four_tiles("L1_cond_cW2", t), tiled, [w[:, 4 * t:4 * t + 4, :] for w in cw2]))
        for t in range(2 * KD):
            pieces.append((rows("L1_cond_mW1", t), wide, [w[:, t, :] for w in mw1]))
        for t in range(2):
            pieces.append((four_tiles("L1_cond_mW2", t), tiled, [w[:, 4 * t:4 * t + 4, :] for w in mw2]))

        def filling(p):
            return (p + 2) % STAGE, (p + 2) // STAGE + 1

        down_w = {0: "L0_cond_W_down", 2: "L2_cond_W_down", 3: "L3_cond_W_down"}
        up_w = {0: "L0_cond_W_up", 2: "L2_cond_W_up", 3: "L3_cond_W_up"}

        block = ctx.enter_context(nc.Block())

        @block.sync
        def _(sp):
            sp.dma_start(roles_i[:, :], a["itok_B_1_2"].partition_broadcast(P)).then_inc(ids_in, 16)
            sp.dma_start(role_col_i[:, 0:1], a["itok_B_1_2"].rearrange("(b o) -> b o", o=1)).then_inc(ids_in, 16)
            sp.dma_start(role_col_i[:, 1:2], a["itok_B_17_1546"].rearrange("(b o) -> b o", o=1)).then_inc(ids_in, 16)
            for n, pair in enumerate((("L1_cond_Wq", "L1_cond_Wk"), ("L1_cond_Wv", "L1_cond_Wp"))):
                for m, w in enumerate(pair):
                    sp.dma_start(tiled(n)[:, KD * m:KD * (m + 1), :],
                                 a[w].rearrange("(k p) n -> p k n", p=P)).then_inc(stage_in[n], 16)

            def piece(p):
                slot, _ = filling(p)
                src, view, _ = pieces[p]
                if p == 1:
                    sp.wait_ge(wT_ps, 2)
                elif p == 2:
                    sp.wait_ge(fold_ps, KD)
                elif p > 2:
                    sp.wait_ge(w_ready, p - STAGE + 1)
                sp.dma_start(view(slot), src).then_inc(stage_in[slot], 16)

            role = []

            def adapter_weights(layer, c):
                if layer == 3:
                    slot, down, up, done = c % WSLOTS, wdB, wuB, wB_in
                    if c >= WSLOTS:
                        sp.wait_ge(upB_ps, c - WSLOTS + 1)
                else:
                    i = lane_a(layer, c)
                    slot, down, up, done = i % WSLOTS, wdA, wuA, wA_in
                    if i >= WSLOTS:
                        sp.wait_ge(upA_ps, i - WSLOTS + 1)
                r = role[c]
                sp.dma_start(down[slot][:, :, :],
                             a[down_w[layer]].rearrange("r (k p) n -> r p k n", p=P)[bass.ds(r, 1), :, :, :]
                             .rearrange("r p k n -> (r p) k n")).then_inc(done[slot], 16)
                sp.dma_start(up[slot][:, :],
                             a[up_w[layer]][bass.ds(r, 1), :, :].rearrange("r p n -> (r p) n")).then_inc(done[slot], 16)

            sp.wait_ge(constants, 1)
            for n, w in enumerate(("L0_cond_b_up", "L2_cond_b_up", "L3_cond_b_up")):
                sp.dma_start(bu_rows[32 * n:32 * n + R, :], a[w]).then_inc(bu_in, 16)
            sp.wait_ge(chunks_ready, 1)
            for c in range(CHUNKS):
                role.append(sp.value_load(chunk_role_i[0:1, c:c + 1], min_val=0, max_val=R - 1))
                adapter_weights(0, c)
                if c in (1, 4, 6, 8):
                    piece((1, 4, 6, 8).index(c))
            for name, w in (("gamma3", "L3_cond_ln_w"), ("beta3", "L3_cond_ln_b")):
                sp.dma_start(table[name][:, :, :], a[w].partition_broadcast(P)).then_inc(tables_in, 16)
            for c in range(WSLOTS):
                adapter_weights(2, c)
                adapter_weights(3, c)
            for p in range(4, len(pieces)):
                piece(p)
            for c in range(WSLOTS, CHUNKS):
                adapter_weights(2, c)
                adapter_weights(3, c)

        @block.tensor
        def _(pe):
            read = [None] * 8

            def take(b, done, value):
                if read[b]:
                    pe.wait_ge(*read[b])
                read[b] = (done, value)

            def split_matmul(dst, w, x, first, last):
                pe.matmul(dst, w[0], x[0], start=first, stop=False)
                pe.matmul(dst, w[0], x[1], start=False, stop=False)
                return pe.matmul(dst, w[1], x[0], start=False, stop=last)

            def vectors():
                pe.wait_ge(constants, 1)
                pe.wait_ge(vectors_in, 12 * 16)
                take(0, vectors_ready, 1)
                pe.transpose(bank[0][:, 0:ROWS], vec_rows[:, :], ident[0:ROWS, 0:ROWS]).then_inc(vectors_ps, 1)

            def find_order():
                pe.wait_ge(sorts_ready, 1)
                pe.wait_ge(spread_ready, 1)
                take(1, order_ready, 1)
                for n in range(2):
                    mm = pe.matmul(bank[1][:, n * POS:(n + 1) * POS], spread[:, n, :], sorts[:, :],
                                   start=True, stop=True)
                mm.then_inc(order_ps, 1)

            def fold_transpose(part):
                pe.wait_ge(constants, 1)
                for n, (slot, half) in ((0, (0, 0)), (1, (0, 1))) if part == 0 else ((2, (1, 0)),):
                    pe.wait_ge(stage_in[slot], 32)
                    take(2 + n, wT_ready, n + 1)
                    for i in range(KD):
                        for t in range(KD):
                            tr = pe.transpose(bank[2 + n][:, t * D + i * P:t * D + (i + 1) * P],
                                              tiled(slot)[:, KD * half + i, t * P:(t + 1) * P], ident[:, :])
                    tr.then_inc(wT_ps, 1)

            def fold(n):
                left, right = (("q", "k"), ("v", None))[n]
                take(2 * n + 1, fold_ready, n + 1)
                pe.wait_ge(wT_ready, 2 + n)
                for m in range(KD):
                    for t in range(KD):
                        moving = wT[right][:, t, :] if right else tiled(1)[:, KD + t, :]
                        mm = pe.matmul(bank[2 * n + 1][:, m * D:(m + 1) * D], wT[left][:, t, m * P:(m + 1) * P],
                                       moving, start=(t == 0), stop=(t == KD - 1))
                mm.then_inc(fold_ps, 1)

            def load(layer, c):
                if layer:
                    return
                b = chain_bank(0, c)
                take(b, sumA_ready, c + 1)
                pe.wait_ge(x_in[c % TSLOTS], 16 * (c // TSLOTS + 1))
                for m in range(KD):
                    tr = pe.transpose(bank[b][:, m * P:(m + 1) * P], x_tok[c % TSLOTS][:, m * P:(m + 1) * P], ident[:, :])
                tr.then_inc(xT_ps, 1)

            def down(layer, c):
                b = chain_bank(layer, c)
                if layer == 3:
                    take(b, sumB_ready, c + 1)
                    pe.wait_ge(wB_in[c % WSLOTS], 32 * (c // WSLOTS + 1))
                    pe.wait_ge(zB_ready, c + 1)
                    w, x, done = wdB[c % WSLOTS], zB[c % XSLOTS], downB_ps
                else:
                    i = lane_a(layer, c)
                    if layer == 2:
                        take(b, sumA_ready, i + 1)
                    pe.wait_ge(wA_in[i % WSLOTS], 32 * (i // WSLOTS + 1))
                    pe.wait_ge(xA_ready, i + 1)
                    w, x, done = wdA[i % WSLOTS], xA[i % XSLOTS], downA_ps
                if layer:
                    for m in range(KD):
                        pe.transpose(bank[b][:, m * P:(m + 1) * P], x[:, m, :], ident[:, :])
                for k in range(KD):
                    mm = pe.matmul(bank[b][:, D:D + P], w[:, k, :], x[:, k, :], start=(k == 0), stop=(k == KD - 1))
                mm.then_inc(done, 1)

            def up(layer, c):
                dst = bank[chain_bank(layer, c)][:, 0:D]
                if layer == 3:
                    pe.wait_ge(resB_ready, c + 1)
                    h, w, done = hB[c % XSLOTS], wuB[c % WSLOTS], upB_ps
                else:
                    i = lane_a(layer, c)
                    pe.wait_ge(hA_ready if layer == 0 else resA_ready, c + 1)
                    h, w, done = hA[i % XSLOTS], wuA[i % WSLOTS], upA_ps
                if c == 0 and layer == 0:
                    pe.wait_ge(bu_ready, 1)
                    pe.wait_ge(hot_ready, 1)
                lo = 32 * (0, 2, 3).index(layer)
                pe.matmul(dst, hot[lo:lo + R, c, :], bu[0][lo:lo + R, :], start=True, stop=False)
                pe.matmul(dst, hot[lo:lo + R, c, :], bu[1][lo:lo + R, :], start=False, stop=False)
                pe.matmul(dst, h[:, :], w[:, :], start=False, stop=True).then_inc(done, 1)

            def turn(layer, c):
                b, i = turn_bank(layer, c), lane_a(layer, c)
                take(b, *((x1_window, KD * (c + 1)) if layer == 0 else (zB_ready, c + 1)))
                pe.wait_ge(normA_ready, i + 1)
                for m in range(KD):
                    tr = pe.transpose(bank[b][:, m * P:(m + 1) * P], yA[i % YSLOTS][:, m * P:(m + 1) * P], ident[:, :])
                tr.then_inc(normA_T_ps, 1)

            def windows_done(h):
                pe.wait_ge(x1_window, KD * (6 if h == 0 else CHUNKS))

            def tokens(h):
                windows_done(h)
                for q in range(2):
                    take(2 + q, tokens_ready, 2 * h + q + 1)
                    for n in range(2):
                        for m in range(KD):
                            lo = h * HALF + (2 * q + n) * P
                            tr = pe.transpose(bank[2 + q][:, n * D + m * P:n * D + (m + 1) * P],
                                              x1T[:, m, lo:lo + P], ident[:, :])
                    tr.then_inc(tokens_ps, 1)

            def pair(w, x, done, read_by, h):
                for m in range(KD):
                    take(m, read_by, KD * h + m + 1)
                    for k in range(KD):
                        mm = split_matmul(bank[m][:, :], [v[:, k, m * P:(m + 1) * P] for v in w],
                                          [v[:, k, :] for v in x], k == 0, k == KD - 1)
                    mm.then_inc(done, 1)

            def project(h):
                pe.wait_ge(fold_ready, 1)
                pe.wait_ge(x1_split, h + 1)
                pair(wqk, x1, project_ps, y_ready, h)

            def scores(h):
                pe.wait_ge(y_ready, KD * (h + 1))
                take(2, dots_copied, h + 1)
                for n in range(G):
                    for k in range(KD):
                        mm = pe.matmul(bank[2][:, n * P:(n + 1) * P], y_T[:, k, n * P:(n + 1) * P],
                                       x1T[:, k, h * HALF + n * P:h * HALF + (n + 1) * P],
                                       start=(k == 0), stop=(k == KD - 1))
                mm.then_inc(scores_ps, 1)

            def mix(h):
                pe.wait_ge(tokens_ready, 2 * (h + 1))
                pe.wait_ge(probs_ready, h + 1)
                for m in range(KD):
                    take(m, z_ready, KD * h + m + 1)
                    for n in range(G):
                        mm = pe.matmul(bank[m][:, n * P:(n + 1) * P], x1_tok[:, n, m * P:(m + 1) * P],
                                       probs_T[:, n, :], start=True, stop=True)
                    mm.then_inc(mix_ps, 1)

            def attend(h):
                pe.wait_ge(fold_ready, 2)
                pe.wait_ge(z_ready, KD * (h + 1))
                pair(wvp, z, attend_ps, ao_ready, h)

            def hidden(phase, j):
                (h, cols), n = half_of(phase), phase * JT + j
                b = ring_bank(phase, j)
                take(b, g_high, n + 1)
                if phase < 2:
                    pe.wait_ge(w_ready, KD)
                    pe.wait_ge(ao_ready, KD * (h + 1))
                    w, x = cw1, [(ao[h], k) for k in range(KD)]
                else:
                    pe.wait_ge(w_ready, 8)
                    pe.wait_ge(cms_ready, KD * (h + 1))
                    w, x = mw1, [(ao[h], k) for k in range(KD)] + [(cms[h], k) for k in range(KD)]
                for k, (v, kk) in enumerate(x):
                    mm = split_matmul(bank[b][:, 0:PHASES[phase][1]], [u[:, k, j * P:(j + 1) * P] for u in w],
                                      [u[:, kk, cols] for u in v], k == 0, k == len(x) - 1)
                mm.then_inc(hidden_ps, 1)

            def outer(phase, part):
                w = cw2 if phase < 2 else mw2
                if part == 0:
                    for m in range(KD):
                        if phase < 2:
                            take(m, cms_full_ready, KD * phase + m + 1)
                        else:
                            take(m, x2_sum, KD * (phase - 2) + m + 1)
                    pe.wait_ge(w_ready, 4 if phase < 2 else 10)
                tiles = range(JT) if phase < 3 else range(2 * part, 2 * part + 2)
                width = PHASES[phase][1]
                for k in tiles:
                    pe.wait_ge(g_ready, phase * JT + k + 1)
                    for m in range(KD):
                        mm = split_matmul(bank[m][:, 0:width], [v[:, k, m * P:(m + 1) * P] for v in w],
                                          [v[:, k, 0:width] for v in g], k == 0, k == JT - 1)
                        if k == JT - 1:
                            mm.then_inc(outer_ps, 1)

            do = {"vectors": vectors, "order": find_order, "fold_transpose": fold_transpose, "fold": fold,
                  "load": load, "down": down, "up": up, "turn": turn, "tokens": tokens, "project": project, "scores": scores, "mix": mix, "attend": attend,
                  "hidden": hidden, "outer": outer}
            for name, *args in steps:
                if name in do:
                    do[name](*args)

        @block.scalar
        def _(act):
            act.wait_ge(constants, 2)
            act.wait_ge(ids_in, 48)
            act.copy(spread[:, 0, :], part_col[0:B, :].to_broadcast([B, P]))
            act.copy(spread[:, 1, :], role_col_i[:, 1:2].to_broadcast([B, P])).then_inc(spread_ready, 1)
            for kind, w in enumerate(("L0_cond_b_down", "L2_cond_b_down", "L3_cond_b_down")):
                act.dma_start(vec_rows[R * kind:R * (kind + 1), :], a[w]).then_inc(vectors_in, 16)
            for v, w in ((GAMMA0, "L0_cond_gamma"), (BETA0, "L0_cond_beta"), (GAMMA2, "L2_cond_gamma"),
                         (BETA2, "L2_cond_beta")):
                act.dma_start(vec_rows[R * v:R * (v + KD), :],
                              a[w].rearrange("r (m f) -> (r m) f", f=P)).then_inc(vectors_in, 16)

            first_tok = []

            def vectors():
                act.wait_ge(hot_col_ready, 1)
                act.copy(hot[:, :, :], hot_col[:, :].unsqueeze(2).to_broadcast([P, CHUNKS, P])).then_inc(hot_ready, 1)
                act.wait_ge(chunks_ready, 1)
                for c in range(CHUNKS):
                    first_tok.append(act.value_load(start_tok_i[0:1, c:c + 1], min_val=0, max_val=N))
                act.wait_ge(vectors_ps, 1)
                act.copy(vecs[:, :], bank[0][:, 0:ROWS]).then_inc(vectors_ready, 1)

            def find_order():
                act.wait_ge(order_ps, 1)
                act.copy(order[:, :, :].rearrange("p a b -> p (a b)"), bank[1][:, 0:2 * POS]).then_inc(order_ready, 1)
                for row, w, n in ((BP, "L1_cond_bp", KD), (CB1, "L1_cond_cb1", JT), (CB2, "L1_cond_cb2", KD),
                                  (MB1, "L1_cond_mb1", JT), (MB2, "L1_cond_mb2", KD)):
                    act.dma_start(vec_rows[row:row + n, :], a[w].rearrange("(n p) -> n p", p=P)).then_inc(vectors_in, 16)

            def fold_transpose(part):
                for n, w in ((0, "q"), (1, "k")) if part == 0 else ((2, "v"),):
                    act.wait_ge(wT_ps, n + 1)
                    act.copy(wT[w][:, :, :].rearrange("p t n -> p (t n)"), bank[2 + n][:, :]).then_inc(wT_ready, 1)

            def fold(n):
                act.wait_ge(fold_ps, n + 1)
                act.copy((wqk, wvp)[n][0][:, :, :].rearrange("p k n -> p (k n)"), bank[2 * n + 1][:, :]).then_inc(fold_high, 1)

            def load(layer, c):
                if layer:
                    return
                act.wait_ge(xT_ps, c + 1)
                if c >= XSLOTS:
                    act.wait_ge(downA_ps, c - XSLOTS + 1)
                act.copy(xA[c % XSLOTS][:, :, :].rearrange("p k n -> p (k n)"),
                         bank[chain_bank(0, c)][:, 0:D]).then_inc(xA_ready, 1)

            def down(layer, c):
                src = bank[chain_bank(layer, c)][:, D:D + P]
                if layer == 3:
                    act.wait_ge(downB_ps, c + 1)
                    if c >= XSLOTS:
                        act.wait_ge(upB_ps, c - XSLOTS + 1)
                    if c >= YSLOTS:
                        act.wait_ge(out_done[c % YSLOTS], 16 * (c // YSLOTS))
                    dst, done = hB[c % XSLOTS], None
                else:
                    i = lane_a(layer, c)
                    act.wait_ge(downA_ps, i + 1)
                    if i >= XSLOTS:
                        act.wait_ge(upA_ps, i - XSLOTS + 1)
                    dst, done = hA[i % XSLOTS], hA_ready if layer == 0 else None
                if layer == 0 and c == 0:
                    act.wait_ge(chunk_vecs_ready, 1)
                ins = act.activation(dst[:, :], src, ACT.Gelu, bias=chunk_vecs[:, BD[(0, 2, 3).index(layer)], c:c + 1])
                if done is not None:
                    ins.then_inc(done, 1)
                if layer:
                    i, y, done = (c, yB, resB_ready) if layer == 3 else (lane_a(2, c), yA, resA_ready)
                    if layer == 2:
                        act.wait_ge(normA_T_ps, i - YSLOTS + 1)
                    act.copy(y[i % YSLOTS][:, :], bank[chain_bank(layer, c)][:, 0:D]).then_inc(done, 1)

            def turn0(c):
                act.wait_ge(normA_T_ps, c + 1)
                if c == 0:
                    act.wait_ge(constants, 3)
                else:
                    act.wait_ge(x1_window, KD * c)
                for m in range(KD):
                    src = bank[turn_bank(0, c)][:, m * P:(m + 1) * P]
                    ins = act.activation(x1T[:, m, bass.ds(first_tok[c], P)], src, ACT.Identity,
                                         bias=chunk_vecs[:, BETA0 + m, c:c + 1],
                                         scale=chunk_vecs[:, GAMMA0 + m, c:c + 1])
                    ins.then_inc(x1_window, 1)

            def turn2(c):
                act.wait_ge(normA_T_ps, lane_a(2, c) + 1)
                if c >= XSLOTS:
                    act.wait_ge(downB_ps, c - XSLOTS + 1)
                for m in range(KD):
                    ins = act.activation(zB[c % XSLOTS][:, m, :], bank[turn_bank(2, c)][:, m * P:(m + 1) * P],
                                         ACT.Identity, bias=chunk_vecs[:, BETA2 + m, c:c + 1],
                                         scale=chunk_vecs[:, GAMMA2 + m, c:c + 1])
                ins.then_inc(zB_ready, 1)

            def tokens(h):
                if h:
                    act.wait_ge(mix_ps, KD * h)
                for q in range(2):
                    act.wait_ge(tokens_ps, 2 * h + q + 1)
                    act.copy(x1_tok[:, 2 * q:2 * q + 2, :].rearrange("p g n -> p (g n)"),
                             bank[2 + q][:, :]).then_inc(tokens_ready, 1)

            def project(h):
                if h:
                    act.wait_ge(scores_ps, h)
                for m in range(KD):
                    act.wait_ge(project_ps, KD * h + m + 1)
                    act.copy(y_T[:, m, :], bank[m][:, :]).then_inc(y_ready, 1)

            def scores(h):
                act.wait_ge(dots_ready, h + 1)
                act.activation(weighed[:, :, :].rearrange("p g n -> p (g n)"),
                               dots[:, :, :].rearrange("p g n -> p (g n)"), ACT.Exp, scale=SCALE).then_inc(exp_ready, 1)

            def mix(h):
                if h:
                    act.wait_ge(attend_ps, KD * h)
                for m in range(KD):
                    act.wait_ge(mix_ps, KD * h + m + 1)
                    act.copy(z[0][:, m, :], bank[m][:, :]).then_inc(z_high, 1)

            def attend(h):
                for m in range(KD):
                    act.wait_ge(attend_ps, KD * h + m + 1)
                    act.activation(ao[h][0][:, m, :], bank[m][:, :], ACT.Identity,
                                   bias=vecs[:, BP + m:BP + m + 1]).then_inc(ao_high, 1)

            def hidden(phase, j):
                n, width = phase * JT + j, PHASES[phase][1]
                b = ring_bank(phase, j)
                act.wait_ge(hidden_ps, n + 1)
                bias = vecs[:, (CB1 if phase < 2 else MB1) + j:(CB1 if phase < 2 else MB1) + j + 1]
                if n >= 2:
                    act.wait_ge(g_ready, n - 1)
                act.activation(g_full[n % 2][:, 0:width], bank[b][:, 0:width], ACT.Gelu, bias=bias)
                if phase and j == 0:
                    act.wait_ge(outer_ps, KD * phase)
                act.activation(g[0][:, j, 0:width], bank[b][:, 0:width], ACT.Gelu,
                               bias=bias).then_inc(g_high, 1)

            def outer(phase, part):
                if phase < 2:
                    if phase:
                        act.wait_ge(outer_ps, 2 * KD)
                    for m in range(KD):
                        act.wait_ge(cms_full_ready, KD * phase + m + 1)
                        act.copy(cms[phase][0][:, m, :], cms_full[:, m, :]).then_inc(cms_high, 1)

            do = {"vectors": vectors, "order": find_order, "fold_transpose": fold_transpose, "fold": fold,
                  "load": load, "down": down, "turn": lambda layer, c: (turn2 if layer else turn0)(c), "tokens": tokens,
                  "project": project, "scores": scores, "mix": mix, "attend": attend,
                  "hidden": hidden, "outer": outer}
            for name, *args in steps:
                if name in do:
                    do[name](*args)

        @block.vector
        def _(dve):
            own = [0]

            def link(ins):
                own[0] += 1
                ins.then_inc(dve_own, 1)
                dve.wait_ge(dve_own, own[0])

            def find_windows():
                dve.wait_ge(constants, 2)
                link(dve.tensor_scalar(past[:, :], seq_from[:, :], part_col[:, 0:1], None, ALU.is_le))
                link(dve.tensor_reduce(seq_col[:, :], past[:, :], X_AXIS, ALU.add))
                dve.scalar_tensor_tensor(out=tok_col[:, :], in0=seq_col[:, :], scalar=-float(S), in1=part_col[:, :],
                                         op0=ALU.mult, op1=ALU.add)
                dve.tensor_scalar(tok_spare[:, :], seq_col[:, :], -float(S), -float(N), ALU.mult, ALU.add)
                dve.wait_ge(ids_in, 48)
                link(dve.tensor_scalar(roles[:, :], roles_i[:, :], 0.0, float(R - 1), ALU.max, ALU.min))
                link(dve.tensor_scalar(key_col[:, 0:1], role_col_i[:, 0:1], 0.0, float(R - 1), ALU.max, ALU.min))
                link(dve.tensor_scalar(key_col[:, 0:1], key_col[:, 0:1], float(B), part_col[0:B, :], ALU.mult, ALU.add))
                link(dve.scalar_tensor_tensor(out=keys[:, :], in0=roles[:, :], scalar=float(B),
                                              in1=pos_row[:, 0:B], op0=ALU.mult, op1=ALU.add))
                link(dve.tensor_scalar(below[:, :], keys[0:B, :], key_col[:, 0:1], None, ALU.is_lt))
                link(dve.tensor_reduce(pos_col[:, :], below[:, :], X_AXIS, ALU.add))
                dve.tensor_scalar(sorts[:, :], pos_row[0:B, :], pos_col[:, 0:1], None,
                                  ALU.is_equal).then_inc(sorts_ready, 1)
                link(dve.tensor_tensor(is_role[:, :, :], roles[:, :].unsqueeze(1).to_broadcast([P, R, B]),
                                       role_row[:, :, :], ALU.is_equal))
                link(dve.tensor_reduce(count[:, :], is_role[:, :, :], X_AXIS, ALU.add))
                link(dve.tensor_tensor(more[:, :, :], count[:, :].unsqueeze(2).to_broadcast([P, R, 8]),
                                       four_row[:, :, :], ALU.is_gt))
                link(dve.tensor_reduce(wins[:, :], more[:, :, :], X_AXIS, ALU.add))
                dve.tensor_scalar(ends4[:, 0:1], wins[:, 0:1], float(WB), None, ALU.mult)
                dve.scalar_tensor_tensor(out=short[:, :], in0=wins[:, 0:2], scalar=-float(WB),
                                         in1=count[:, 0:2], op0=ALU.mult, op1=ALU.add)
                link(dve.tensor_scalar(ends4[:, 1:2], wins[:, 1:2], wins[:, 0:1], float(WB), ALU.add, ALU.mult))
                link(dve.tensor_tensor(later[:, :, :], chunk4_row[:, :].unsqueeze(1).to_broadcast([P, 2, CHUNKS]),
                                       ends4[:, :].unsqueeze(2).to_broadcast([P, 2, CHUNKS]), ALU.is_ge))
                link(dve.tensor_tensor(chunk_role[:, :], later[:, 0, :], later[:, 1, :], ALU.add))
                dve.tensor_copy(chunk_role_i[:, :], chunk_role[:, :])
                dve.tensor_scalar(hot_col[:, :], chunk_role[:, :], tok_col[:, 0:1], None,
                                  ALU.is_equal).then_inc(hot_col_ready, 1)
                link(dve.scalar_tensor_tensor(out=start[:, :], in0=later[:, 0, :], scalar=short[:, 0:1],
                                              in1=chunk4_row[:, :], op0=ALU.mult, op1=ALU.add))
                link(dve.scalar_tensor_tensor(out=start[:, :], in0=later[:, 1, :], scalar=short[:, 1:2],
                                              in1=start[:, :], op0=ALU.mult, op1=ALU.add))
                link(dve.tensor_scalar(start[:, :], start[:, :], float(B), None, ALU.min))
                dve.tensor_scalar(start_tok_i[:, :], start[:, :], float(S), None, ALU.mult).then_inc(chunks_ready, 1)
                link(dve.tensor_tensor(reach[:, :, :], pos_row[:, :].unsqueeze(1).to_broadcast([P, CHUNKS, POS]),
                                       start[:, :].unsqueeze(2).to_broadcast([P, CHUNKS, POS]), ALU.subtract))

            def find_order():
                dve.wait_ge(order_ready, 1)
                link(dve.scalar_tensor_tensor(out=reach[:, :, :], in0=reach[:, :, :], scalar=seq_col[:, 0:1],
                                              in1=order[:, 0, :].unsqueeze(1).to_broadcast([P, CHUNKS, POS]),
                                              op0=ALU.is_equal, op1=ALU.mult))
                link(dve.tensor_reduce(seq_at[:, :], reach[:, :, :], X_AXIS, ALU.add))
                dve.tensor_scalar(from_row_i[:, :], seq_at[:, :], float(S), tok_col[:, 0:1],
                                  ALU.mult, ALU.add).then_inc(rows_in_ready, 1)
                link(dve.tensor_scalar(end[:, :], later[:, 0, :], count[:, 1:2], count[:, 0:1], ALU.mult, ALU.add))
                link(dve.scalar_tensor_tensor(out=end[:, :], in0=later[:, 1, :], scalar=count[:, 2:3],
                                              in1=end[:, :], op0=ALU.mult, op1=ALU.add))
                dve.scalar_tensor_tensor(out=valid[:, :], in0=start[:, :], scalar=seq_col[:, 0:1], in1=end[:, :],
                                         op0=ALU.add, op1=ALU.is_lt)
                link(dve.tensor_scalar(row_at[:, :], seq_at[:, :], float(S), tok_spare[:, 0:1], ALU.mult, ALU.add))
                link(dve.tensor_tensor(row_at[:, :], row_at[:, :], valid[:, :], ALU.mult))
                dve.tensor_scalar(row_at_i[:, :], row_at[:, :], spare_col[:, 0:1], None, ALU.add).then_inc(rows_ready, 1)

            def vectors():
                dve.wait_ge(bu_in, 48)
                dve.tensor_copy(bu[0][0:2 * 32 + R, :], bu_rows[0:2 * 32 + R, :]).then_inc(bu_high, 1)
                dve.wait_ge(bu_high, 1)
                dve.tensor_tensor(bu[1][0:2 * 32 + R, :], bu_rows[0:2 * 32 + R, :],
                                  bu[0][0:2 * 32 + R, :].bitcast(F32), ALU.subtract).then_inc(bu_ready, 1)
                dve.wait_ge(vectors_ready, 1)
                link(dve.tensor_tensor(role_hot[:, :, :], chunk_role[:, :].unsqueeze(2).to_broadcast([P, CHUNKS, R]),
                                       role_in[:, :, :], ALU.is_equal))
                for v in range(PER_ROLE):
                    mine = (vecs[:, R * v:R * (v + 1)] if v in BD else
                            vecs[:, R * GAMMA0:BP].rearrange("p (v r m) -> p v m r", r=R, m=KD)
                            [:, (v - GAMMA0) // KD, (v - GAMMA0) % KD, :])
                    ins = dve.tensor_tensor(picked[:, v, :, :], role_hot[:, :, :],
                                            mine.unsqueeze(1).to_broadcast([P, CHUNKS, R]), ALU.mult)
                link(ins)
                dve.tensor_reduce(chunk_vecs[:, :, :], picked[:, :, :, :], X_AXIS, ALU.add).then_inc(chunk_vecs_ready, 1)
                for m in range(KD):
                    ins = dve.tensor_scalar(target[:, m, :], order[:, 1, :], (part_col, part_col2)[m][:, 0:1],
                                            vecs[:, CB2 + m:CB2 + m + 1], ALU.is_equal, ALU.add)
                ins.then_inc(target_ready, 1)

            def fold(n):
                dve.wait_ge(fold_high, n + 1)
                w = (wqk, wvp)[n]
                dve.tensor_tensor(w[1][:, :, :].rearrange("p k n -> p (k n)"), bank[2 * n + 1][:, :],
                                  w[0][:, :, :].rearrange("p k n -> p (k n)").bitcast(F32),
                                  ALU.subtract).then_inc(fold_ready, 1)

            def weights(p):
                slot, fill = filling(p)
                _, view, parts = pieces[p]
                if p == 4:
                    dve.wait_ge(attend_ps, 2 * KD)
                if p == 8:
                    dve.wait_ge(hidden_ps, 2 * JT)
                dve.wait_ge(stage_in[slot], 16 * fill + (16 if slot < 2 else 0))
                dve.tensor_copy(parts[0], view(slot)).then_inc(w_high, 1)
                if p < DVE_PIECES:
                    dve.wait_ge(w_high, p + 1)
                    dve.tensor_tensor(parts[1], view(slot), parts[0].bitcast(F32), ALU.subtract).then_inc(w_ready, 1)

            def moments(y, x, st, mv, k, bank_ap, done, summed, n):
                dve.tensor_tensor(y, bank_ap, x, ALU.add).then_inc(summed, 1)
                dve.wait_ge(summed, n + 1)
                link(dve.bn_stats(st[:, k, :], y))
                dve.bn_aggr(mv[:, k, :], st[:, k, :]).then_inc(done, 1)

            first_tok, role = [], []

            def load(layer, c):
                if layer == 0:
                    return
                i = lane_a(2, c)
                dve.wait_ge(x2_ready, KD * first_final(c))
                dve.wait_ge(downA_ps, i - XSLOTS + 1)
                dve.tensor_copy(xA[i % XSLOTS][:, :, :], x1T[:, :, bass.ds(first_tok[c], P)]).then_inc(xA_ready, 1)

            def up(layer, c):
                if layer == 3:
                    k = c % YSLOTS
                    y = yB[k][:, :]
                    dve.wait_ge(upB_ps, c + 1)
                    moments(y, y, statsB, mvB, k, bank[chain_bank(3, c)][:, 0:D], varB_ready, sumB_ready, c)
                else:
                    i = lane_a(layer, c)
                    k = i % YSLOTS
                    y = yA[k][:, :]
                    if layer == 0 and c >= YSLOTS:
                        dve.wait_ge(normA_T_ps, c - YSLOTS + 1)
                    dve.wait_ge(upA_ps, i + 1)
                    moments(y, x_tok[c % TSLOTS][:, :] if layer == 0 else y, statsA, mvA, k,
                            bank[chain_bank(layer, c)][:, 0:D], varA_ready, sumA_ready, i)

            def center(layer, c):
                i = lane_a(layer, c)
                k = i % YSLOTS
                dve.wait_ge(rstdA_ready, i + 1)
                dve.tensor_scalar(yA[k][:, :], yA[k][:, :], mvA[:, k, 0:1], rstdA[:, k, 1:2],
                                  ALU.subtract, ALU.mult).then_inc(normA_ready, 1)

            def finish(layer, c):
                k = c % YSLOTS
                r = role[c]
                if c == 0:
                    dve.wait_ge(tables_in, 2 * 16)
                dve.wait_ge(rstdB_ready, c + 1)
                link(dve.scalar_tensor_tensor(out=yB[k][:, :], in0=yB[k][:, :], scalar=mvB[:, k, 0:1],
                                              in1=table["gamma3"][:, bass.ds(r, 1), :].rearrange("p r n -> p (r n)"),
                                              op0=ALU.subtract, op1=ALU.mult))
                dve.scalar_tensor_tensor(out=yB[k][:, :], in0=yB[k][:, :], scalar=rstdB[:, k, 1:2],
                                         in1=table["beta3"][:, bass.ds(r, 1), :].rearrange("p r n -> p (r n)"),
                                         op0=ALU.mult, op1=ALU.add).then_inc(out_ready, 1)

            def project(h):
                dve.wait_ge(x1_window, KD * (6 if h == 0 else CHUNKS))
                if h:
                    dve.wait_ge(project_ps, KD * h)
                src = x1T[:, :, h * HALF:(h + 1) * HALF]
                link(dve.tensor_copy(x1[0][:, :, :], src))
                dve.tensor_tensor(x1[1][:, :, :], src, x1[0][:, :, :].bitcast(F32), ALU.subtract).then_inc(x1_split, 1)

            def scores(h):
                dve.wait_ge(scores_ps, h + 1)
                for q in range(WB):
                    lo, hi = S * q, S * (q + 1)
                    src = bank[2][lo:hi, :].rearrange("p (g n) -> p g n", n=P)
                    ins = dve.tensor_copy(dots[lo:hi, :, :], src[:, :, lo:hi])
                ins.then_inc(dots_copied, 1)
                dve.wait_ge(dots_copied, h + 1)
                link(dve.tensor_reduce(peak[:, :], dots[:, :, :], X_AXIS, ALU.max))
                dve.tensor_tensor(dots[:, :, :], dots[:, :, :], peak[:, :].unsqueeze(2).to_broadcast([P, G, S]),
                                  ALU.subtract).then_inc(dots_ready, 1)

            def mix(h):
                dve.wait_ge(exp_ready, h + 1)
                link(dve.tensor_reduce(total[:, :], weighed[:, :, :], X_AXIS, ALU.add))
                link(dve.reciprocal(inv_total[:, :], total[:, :]))
                link(dve.tensor_tensor(probs[:, :, :], weighed[:, :, :],
                                       inv_total[:, :].unsqueeze(2).to_broadcast([P, G, S]), ALU.mult))
                if h:
                    dve.wait_ge(mix_ps, KD * h)
                else:
                    dve.wait_ge(constants, 3)
                for q in range(WB):
                    lo, hi = S * q, S * (q + 1)
                    ins = dve.transpose(probs_T[lo:hi, :, lo:hi], probs[lo:hi, :, :])
                ins.then_inc(probs_ready, 1)
                for m in range(KD):
                    dve.wait_ge(z_high, KD * h + m + 1)
                    dve.tensor_tensor(z[1][:, m, :], bank[m][:, :], z[0][:, m, :].bitcast(F32),
                                      ALU.subtract).then_inc(z_ready, 1)

            def attend(h):
                for m in range(KD):
                    dve.wait_ge(ao_high, KD * h + m + 1)
                    dve.scalar_tensor_tensor(out=ao[h][1][:, m, :], in0=bank[m][:, :],
                                             scalar=vecs[:, BP + m:BP + m + 1], in1=ao[h][0][:, m, :].bitcast(F32),
                                             op0=ALU.add, op1=ALU.subtract).then_inc(ao_ready, 1)

            def hidden(phase, j):
                n, width = phase * JT + j, PHASES[phase][1]
                dve.wait_ge(g_high, n + 1)
                dve.tensor_tensor(g[1][:, j, 0:width], g_full[n % 2][:, 0:width], g[0][:, j, 0:width].bitcast(F32),
                                  ALU.subtract).then_inc(g_ready, 1)
                if n < CHUNKS:
                    first_tok.append(dve.value_load(start_tok_i[0:1, n:n + 1], min_val=0, max_val=N))
                elif n < 2 * CHUNKS:
                    role.append(dve.value_load(chunk_role_i[0:1, n - CHUNKS:n - CHUNKS + 1], min_val=0, max_val=R - 1))

            def outer(phase, part):
                if phase > 2 and part < 3:
                    return
                h = phase % 2
                if phase < 2:
                    if phase == 0:
                        dve.wait_ge(target_ready, 1)
                    else:
                        dve.wait_ge(sum_ready, KD)
                    for m in range(KD):
                        dve.wait_ge(outer_ps, KD * phase + m + 1)
                        dve.tensor_tensor(cms_full[:, m, :].rearrange("p (b s) -> p b s", s=S),
                                          bank[m][:, :].rearrange("p (b s) -> p b s", s=S),
                                          target[:, m, h * (B // 2):(h + 1) * (B // 2)].unsqueeze(2).to_broadcast([P, B // 2, S]),
                                          ALU.add).then_inc(cms_full_ready, 1)
                    for m in range(KD):
                        dve.wait_ge(cms_high, KD * phase + m + 1)
                        dve.tensor_tensor(cms[h][1][:, m, :], cms_full[:, m, :], cms[h][0][:, m, :].bitcast(F32),
                                          ALU.subtract).then_inc(cms_ready, 1)
                else:
                    lo, width = PHASES[phase]
                    dve.wait_ge(sum_ready, KD * (lo // HALF + 1))
                    for m in range(KD):
                        dve.wait_ge(outer_ps, KD * phase + m + 1)
                        part = x1T[:, m, lo:lo + width]
                        dve.scalar_tensor_tensor(out=part, in0=bank[m][:, 0:width],
                                                 scalar=vecs[:, MB2 + m:MB2 + m + 1], in1=part,
                                                 op0=ALU.add, op1=ALU.add).then_inc(x2_sum, 1)
                        dve.wait_ge(x2_sum, KD * (phase - 2) + m + 1)
                        dve.tensor_scalar(part, part, 0.0, 1.0, ALU.max, ALU.min).then_inc(x2_ready, 1)

            find_windows()
            do = {"vectors": lambda: None, "order": lambda: (find_order(), vectors()), "fold": fold,
                  "weights": weights, "load": load, "up": up, "center": center, "finish": finish,
                  "project": project, "scores": scores, "mix": mix, "attend": attend,
                  "hidden": hidden, "outer": outer}
            for name, *args in steps:
                if name in do:
                    do[name](*args)

        @block.gpsimd
        def _(pool):
            own = [0]

            def link(ins):
                own[0] += 1
                ins.then_inc(pool_own, 1)
                pool.wait_ge(pool_own, own[0])

            link(pool.memset(ident[:, :], 0.0))
            link(pool.memset(bu_rows[:, :], 0.0))
            pool.affine_select(out=ident[:, :], in_=ident[:, :], compare_op=ALU.not_equal, fill=1.0, base=0,
                               pattern=[[-1, P]], channel_multiplier=1).then_inc(constants, 1)

            def iota(dst, pattern, base=0, mult=0):
                return pool.iota(dst, pattern, base=base, channel_multiplier=mult,
                                 allow_small_or_imprecise_dtypes=True)

            iota(pos_row[:, :], [[1, POS]])
            iota(part_col[:, :], [[0, 1]], 0, 1)
            iota(role_row[:, :, :], [[1, R], [0, B]])
            iota(four_row[:, :, :], [[0, R], [WB, 8]])
            iota(chunk4_row[:, :], [[WB, CHUNKS]])
            iota(role_in[:, :, :], [[0, CHUNKS], [1, R]])
            iota(part_col2[:, :], [[0, 1]], P, 1)
            iota(spare_col[:, :], [[0, 1]], N, 1)
            pool.memset(power[:, :], -0.5)
            iota(seq_from[:, :], [[S, WB - 1]], S, 0).then_inc(constants, 1)
            pool.memset(x1T[:, :, N:POS * S], 0.0)
            pool.memset(probs_T[:, :, :], 0.0).then_inc(constants, 1)

            def weights(p):
                if p < DVE_PIECES:
                    return
                slot, _ = filling(p)
                _, view, parts = pieces[p]
                if p == DVE_PIECES:
                    pool.wait_ge(w_ready, p)
                pool.wait_ge(w_high, p + 1)
                pool.tensor_tensor(parts[1], view(slot), parts[0].bitcast(F32), ALU.subtract).then_inc(w_ready, 1)

            def gather(c):
                if c >= TSLOTS:
                    pool.wait_ge(sumA_ready, c - TSLOTS + 1)
                pool.indirect_dma_start(
                    out=x_tok[c % TSLOTS][:, :], out_offset=None, in_=a["x"].rearrange("b s d -> (b s) d"),
                    in_offset=bass.IndirectOffsetOnAxis(ap=from_row_i[:, c:c + 1], axis=0)
                    ).then_inc(x_in[c % TSLOTS], 16)

            def find_order():
                pool.wait_ge(rows_in_ready, 1)
                for c in range(TSLOTS):
                    gather(c)

            def rstd(var, mv, k, ready, n, done):
                pool.wait_ge(ready, n)
                link(pool.tensor_scalar(var[:, k, 0:1], mv[:, k, 1:2], LN_EPS, None, ALU.add))
                pool.tensor_tensor(var[:, k, 1:2], var[:, k, 0:1], power[:, :], ALU.pow).then_inc(done, 1)

            def up(layer, c):
                if layer == 3:
                    rstd(rstdB, mvB, c % YSLOTS, varB_ready, c + 1, rstdB_ready)
                else:
                    i = lane_a(layer, c)
                    rstd(rstdA, mvA, i % YSLOTS, varA_ready, i + 1, rstdA_ready)
                if layer == 0 and c + TSLOTS < CHUNKS:
                    gather(c + TSLOTS)

            def finish(layer, c):
                if c == 0:
                    pool.wait_ge(rows_ready, 1)
                pool.wait_ge(out_ready, c + 1)
                pool.indirect_dma_start(
                    out=out.rearrange("b s d -> (b s) d"),
                    out_offset=bass.IndirectOffsetOnAxis(ap=row_at_i[:, c:c + 1], axis=0),
                    in_=yB[c % YSLOTS][:, :], in_offset=None,
                    bounds_check=N - 1, oob_is_err=False).then_inc(out_done[c % YSLOTS], 16)

            def outer(phase, part):
                if phase < 2:
                    for m in range(KD):
                        pool.wait_ge(cms_full_ready, KD * phase + m + 1)
                        half = x1T[:, m, phase * HALF:(phase + 1) * HALF]
                        pool.tensor_tensor(half, half, cms_full[:, m, :], ALU.add).then_inc(sum_ready, 1)

            do = {"order": find_order, "weights": weights, "up": up, "finish": finish, "outer": outer}
            for name, *args in steps:
                if name in do:
                    do[name](*args)
            for k in range(YSLOTS):
                pool.wait_ge(out_done[k], 16 * len(range(k, CHUNKS, YSLOTS)))


def kernel(**inputs):
    import numpy as np
    import concourse.bacc as bacc
    from concourse.bass_utils import run_bass_kernel_spmd

    nc = bacc.Bacc("TRN2", target_bir_lowering=False, num_devices=1)
    arrays, aps = {}, {}
    for name, value in inputs.items():
        if name == "_lenS":
            continue
        v = np.ascontiguousarray(value)
        arrays[f"in_{name}"] = v
        aps[name] = nc.dram_tensor(f"in_{name}", v.shape, mybir.dt.from_np(v.dtype), kind="ExternalInput").ap()
    out = nc.dram_tensor("out", (B, S, D), F32, kind="ExternalOutput").ap()
    build(nc, aps, out)
    return run_bass_kernel_spmd(nc, [arrays], core_ids=[0]).results[0]["out"]
```

```python
from contextlib import ExitStack

import concourse.bass as bass
from concourse import mybir

F32 = mybir.dt.float32
F32R = mybir.dt.float32r
I32 = mybir.dt.int32
U32 = mybir.dt.uint32
ALU = mybir.AluOpType
ACT = mybir.ActivationFunctionType
X_AXIS = mybir.AxisListType.X

P = 128
B, S, D = 32, 32, 256
N = B * S
R = 3
KD = D // P
HID = 4 * D
JT = HID // P
HALF = N // 2
G = HALF // P
WB = P // S
CHUNKS = (B + R * (WB - 1)) // WB
POS = B + WB
HALF_WINDOWS = (B // 2 + R * (WB - 1)) // WB
EARLY = (HALF + HALF // 2) // S // WB
LN_EPS = 1e-5
SCALE = float(D) ** -0.5

BD, GAMMA0, BETA0, GAMMA2, BETA2 = (0, 1, 2), 3, 5, 7, 9
PER_ROLE = 11
BP = PER_ROLE * R
CB1, CB2 = BP + KD, BP + KD + JT
MB1, MB2 = CB2 + KD, CB2 + KD + JT
ROWS = MB2 + KD

XSLOTS, YSLOTS, WSLOTS, TSLOTS = 3, 4, 4, 6
PROJECT_BANKS, SCORE_BANKS = (0, 4), (2, 7)
PHASES = ((0, HALF), (HALF, HALF), (0, HALF), (HALF, HALF // 2), (HALF + HALF // 2, HALF // 2))
STAGE = 3


def plan():
    steps = [("order",), ("fold_transpose", 0), ("fold_transpose", 1), ("vectors",), ("fold", 0, 0), ("load", 0, 0),
             ("fold", 0, 1), ("fold_low", 0)]

    def ticks(stages, t, lo, hi):
        for name, late in stages:
            c = lo + t - late
            if lo <= c < hi:
                steps.append((name[:-1], int(name[-1]), c))

    first = (("up0", 1), ("center0", 2), ("down0", 0), ("load0", -1), ("turn0", 3))
    last_a = (("down2", 0), ("down3", 2), ("center2", 1), ("finish3", 4))
    last_b = (("load2", -1), ("up2", 0), ("turn2", 1), ("up3", 2))

    def tick0(t):
        ticks(first, t, 0, CHUNKS)

    for t in range(9):
        tick0(t)
    steps.extend([("split", 0), ("tokens", 0)])
    tick0(9)
    steps.extend([("project", 0)])
    tick0(10)
    steps.extend([("scores", 0)])
    tick0(11)
    steps.extend([("probs", 0), ("fold", 1, 0), ("fold", 1, 1)])
    tick0(12)
    steps.extend([("fold_low", 1), ("weights", 0), ("split", 1), ("mix", 0), ("tokens", 1), ("project", 1),
                  ("weights", 1), ("attend", 0), ("scores", 1), ("probs", 1), ("weights", 2), ("weights", 3)])
    steps.extend([("hidden", 0, j) for j in range(3)])
    steps.extend([("mix", 1)])
    steps.extend([("hidden", 0, j) for j in range(3, 6)])
    steps.extend([("attend", 1)])
    steps.extend([("hidden", 0, j) for j in range(6, 8)])
    steps.extend([("weights", 4), ("outer", 0, 0), ("weights", 5)])
    for j in range(JT):
        steps.append(("hidden", 1, j))
        if j in (1, 4):
            steps.append(("weights", 6 + (j == 4)))
    steps.extend([("outer", 1, 0), ("weights", 8)])
    for j in range(JT):
        steps.append(("hidden", 2, j))
        if j == 3:
            steps.append(("weights", 9))
    steps.extend([("outer", 2, 0)])

    starts = {0: 0, 1: 1, 2: 2, 3: 3, 4: 6, 5: 7, 6: 11, 7: 12, 8: 13, 9: 14}

    def half_tick(n):
        for name, late in (last_a, last_b)[n % 2]:
            for c, start in starts.items():
                if start == n // 2 - late:
                    steps.append((name[:-1], int(name[-1]), c))

    n = -1
    for phase in (3, 4):
        for unit in [("hidden", phase, j) for j in range(JT)] + [("outer", phase, q) for q in range(4)]:
            steps.append(unit)
            if unit != ("hidden", 3, 0):
                half_tick(n)
                n += 1
    while n < 2 * (starts[CHUNKS - 1] + 5):
        half_tick(n)
        n += 1
    return steps


def build(nc, a, out):
    steps = plan()
    with ExitStack() as ctx:
        at = [(nc.sbuf_base + 31) // 32 * 32]

        def place(name, shape, dt, offset=None):
            size = 4
            for n in shape[1:]:
                size *= n
            size = (size + 31) // 32 * 32
            if offset is None:
                offset = at[0]
                at[0] += size
            return nc.alloc_sbuf_tensor_at(name, shape, dt, offset=offset)

        def sem(name):
            return ctx.enter_context(nc.semaphore(name))

        bank = [ctx.enter_context(nc.psum_tensor(f"bank{b}", [P, 512], F32)) for b in range(8)]

        ident = place("ident", [P, P], F32)
        pos_row = place("pos_row", [P, POS], F32)
        chunk4_row = place("chunk4_row", [P, CHUNKS], F32)
        role_row = place("role_row", [P, R, B], F32)
        four_row = place("four_row", [P, R, 8], F32)
        tok_col = place("tok_col", [P, 1], F32)
        role_in = place("role_in", [P, CHUNKS, R], F32)
        part_col = place("part_col", [P, 1], F32)
        gelu_first = place("gelu_first", [P, 1], F32)
        part_col2 = place("part_col2", [P, 1], F32)
        seq_col = place("seq_col", [P, 1], F32)
        seq_from = place("seq_from", [P, WB - 1], F32)
        past = place("past", [P, WB - 1], F32)
        spare_col = place("spare_col", [P, 1], F32)
        tok_spare = place("tok_spare", [P, 1], F32)
        power = place("power", [P, 1], F32)
        roles_i = place("roles_i", [P, B], I32)
        role_col_i = place("role_col_i", [B, 2], I32)
        roles = place("roles", [P, B], F32)
        keys = place("keys", [P, B], F32)
        key_col = place("key_col", [B, 1], F32)
        below = place("below", [B, B], F32)
        pos_col = place("pos_col", [B, 1], F32)
        sorts = place("sorts", [B, POS], F32)
        spread = place("spread", [B, 2, P], F32)
        is_role = place("is_role", [P, R, B], F32)
        count = place("count", [P, R], F32)
        more = place("more", [P, R, 8], F32)
        wins = place("wins", [P, R], F32)
        ends4 = place("ends4", [P, 2], F32)
        short = place("short", [P, 2], F32)
        later = place("later", [P, 2, CHUNKS], F32)
        chunk_role = place("chunk_role", [P, CHUNKS], F32)
        start = place("start", [P, CHUNKS], F32)
        end = place("end", [P, CHUNKS], F32)
        start_tok_i = place("start_tok_i", [P, CHUNKS], I32)
        chunk_role_i = place("chunk_role_i", [P, CHUNKS], I32)
        codes = place("codes", [P, POS], F32)
        reach = place("reach", [P, CHUNKS, POS], F32)
        seq_at = place("seq_at", [P, CHUNKS], F32)
        from_row_i = place("from_row_i", [P, CHUNKS], U32)
        valid = place("valid", [P, CHUNKS], F32)
        row_at = place("row_at", [P, CHUNKS], F32)
        row_at_i = place("row_at_i", [P, CHUNKS], U32)
        role_hot = place("role_hot", [P, CHUNKS, R], F32)
        vec_rows = place("vec_rows", [ROWS, P], F32)
        vecs = place("vecs", [P, ROWS], F32)
        picked = place("picked", [P, PER_ROLE, CHUNKS, R], F32)
        chunk_vecs = place("chunk_vecs", [P, PER_ROLE, CHUNKS], F32)
        target = place("target", [P, KD, POS], F32)

        stage = [place(f"stage{i}", [P, HID], F32) for i in range(STAGE)]
        wdA = [place(f"wdA{i}", [P, KD, P], F32) for i in range(WSLOTS)]
        wuA = [place(f"wuA{i}", [P, D], F32) for i in range(WSLOTS)]
        wdB = [place(f"wdB{i}", [P, KD, P], F32) for i in range(WSLOTS)]
        wuB = [place(f"wuB{i}", [P, D], F32) for i in range(WSLOTS)]
        xA = [place(f"xA{i}", [P, KD, P], F32) for i in range(XSLOTS)]
        hA = [place(f"hA{i}", [P, P], F32) for i in range(XSLOTS)]
        yA = [place(f"yA{i}", [P, D], F32) for i in range(YSLOTS)]
        zB = [place(f"zB{i}", [P, KD, P], F32) for i in range(XSLOTS)]
        hB = [place(f"hB{i}", [P, P], F32) for i in range(XSLOTS)]
        yB = [place(f"yB{i}", [P, D], F32) for i in range(YSLOTS)]
        statsA = place("statsA", [P, YSLOTS, 6], F32)
        mvA = place("mvA", [P, YSLOTS, 2], F32)
        rstdA = place("rstdA", [P, YSLOTS, 2], F32)
        statsB = place("statsB", [P, YSLOTS, 6], F32)
        mvB = place("mvB", [P, YSLOTS, 2], F32)
        rstdB = place("rstdB", [P, YSLOTS, 2], F32)
        table = {}
        for name in ("gamma3", "beta3"):
            table[name] = place(f"table_{name}", [P, R, D], F32)
        bu_rows = place("bu_rows", [P, D], F32)
        bu_high = place("bu_high", [P, D], F32R)
        bu = place("bu", [P, D], F32R)
        low_row = place("low_row", [P, 1], F32)
        role_row_of = place("role_row_of", [P, 1], F32)
        hot_col = place("hot_col", [P, CHUNKS], F32)
        hot = place("hot", [P, CHUNKS, P], F32R)
        x1T = place("x1T", [P, KD, POS * S], F32)
        cw1_at = at[0]
        cw1 = [place(f"cw1_{x}", [P, KD, HID], F32R) for x in "hl"]
        cw2_at = at[0]
        cw2 = [place(f"cw2_{x}", [P, JT, D], F32R) for x in "hl"]
        mw2 = [place(f"mw2_{x}", [P, JT, D], F32R, cw1_at + n * 4 * JT * D) for n, x in enumerate("hl")]
        ao = [[place(f"ao{h}_{x}", [P, KD, HALF], F32R) for x in "hl"] for h in range(2)]
        g = [place(f"g_{x}", [P, JT, HALF], F32R) for x in "hl"]
        g_full = [place(f"g_full{i}", [P, HALF], F32) for i in range(2)]

        early = at[0]
        x_tok = [place(f"x_tok{i}", [P, D], F32) for i in range(TSLOTS)]
        y_T = place("y_T", [P, KD, HALF], F32, at[0])
        wT = {w: place(f"wT_{w}", [P, KD, D], F32) for w in "qkv"}
        wqk = [place(f"wqk_{x}", [P, KD, D], F32R) for x in "hl"]
        wvp = [place(f"wvp_{x}", [P, KD, D], F32R) for x in "hl"]
        x1 = [place(f"x1_{x}", [P, KD, HALF], F32R) for x in "hl"]
        x1_tok = place("x1_tok", [P, G, D], F32)
        probs_T = place("probs_T", [P, G, P], F32)
        dots = place("dots", [P, G, S], F32)
        weighed = place("weighed", [P, G, S], F32)
        probs = place("probs", [P, G, S], F32)
        peak = place("peak", [P, G], F32)
        total = place("total", [P, G], F32)
        inv_total = place("inv_total", [P, G], F32)
        z = [place(f"z_{x}", [P, KD, HALF], F32R) for x in "hl"]
        early_end = at[0]

        at[0] = early
        mw1 = [place(f"mw1_{x}", [P, 2 * KD, HID], F32R) for x in "hl"]
        cms = [[place(f"cms0_{x}", [P, KD, HALF], F32R) for x in "hl"],
               [place(f"cms1_{x}", [P, KD, HALF], F32R, cw2_at + n * 4 * KD * HALF) for n, x in enumerate("hl")]]
        cms_full = place("cms_full", [P, KD, HALF], F32)
        at[0] = max(at[0], early_end)

        ids_in = sem("ids_in")
        vectors_in = sem("vectors_in")
        mlp_vectors_in = sem("mlp_vectors_in")
        tables_in = sem("tables_in")
        stage_in = [sem(f"stage_in{i}") for i in range(STAGE)]
        wA_in = [sem(f"wA_in{i}") for i in range(WSLOTS)]
        wB_in = [sem(f"wB_in{i}") for i in range(WSLOTS)]
        x_in = [sem(f"x_in{i}") for i in range(TSLOTS)]
        bu_in = sem("bu_in")
        bu_high_ready = sem("bu_high_ready")
        bu_ready = sem("bu_ready")
        hot_ready = sem("hot_ready")
        out_done = [sem(f"out_done{i}") for i in range(YSLOTS)]
        constants = sem("constants")
        dve_own = sem("dve_own")
        pool_own = sem("pool_own")
        sorts_ready = sem("sorts_ready")
        spread_ready = sem("spread_ready")
        order_ps = sem("order_ps")
        chunks_ready = sem("chunks_ready")
        rows_in_ready = sem("rows_in_ready")
        rows_ready = sem("rows_ready")
        vectors_ps = sem("vectors_ps")
        vectors_ready = sem("vectors_ready")
        chunk_vecs_ready = sem("chunk_vecs_ready")
        target_ready = sem("target_ready")
        wT_ps = sem("wT_ps")
        wT_ready = sem("wT_ready")
        fold_ps = sem("fold_ps")
        fold_high = sem("fold_high")
        fold_ready = sem("fold_ready")
        w_high = sem("w_high")
        w_ready = sem("w_ready")
        order_ready = sem("order_ready")
        sumA_ready = sem("sumA_ready")
        sumB_ready = sem("sumB_ready")
        dots_copied = sem("dots_copied")
        xT_ps = sem("xT_ps")
        resA_ready = sem("resA_ready")
        resB_ready = sem("resB_ready")
        xA_ready = sem("xA_ready")
        downA_ps = sem("downA_ps")
        hA_ready = sem("hA_ready")
        upA_ps = sem("upA_ps")
        varA_ready = sem("varA_ready")
        rstdA_ready = sem("rstdA_ready")
        normA_ready = sem("normA_ready")
        normA_T_ps = sem("normA_T_ps")
        x1_window = sem("x1_window")
        zB_ready = sem("zB_ready")
        downB_ps = sem("downB_ps")
        upB_ps = sem("upB_ps")
        varB_ready = sem("varB_ready")
        rstdB_ready = sem("rstdB_ready")
        out_ready = sem("out_ready")
        tokens_ps = sem("tokens_ps")
        tokens_ready = sem("tokens_ready")
        x1_split = sem("x1_split")
        project_ps = sem("project_ps")
        y_ready = sem("y_ready")
        scores_ps = sem("scores_ps")
        dots_ready = sem("dots_ready")
        exp_ready = sem("exp_ready")
        probs_ready = sem("probs_ready")
        mix_ps = sem("mix_ps")
        z_high = sem("z_high")
        z_ready = sem("z_ready")
        attend_ps = sem("attend_ps")
        ao_high = sem("ao_high")
        ao_ready = sem("ao_ready")
        hidden_ps = sem("hidden_ps")
        g_high = sem("g_high")
        g_ready = sem("g_ready")
        outer_ps = sem("outer_ps")
        cms_full_ready = sem("cms_full_ready")
        cms_high = sem("cms_high")
        cms_ready = sem("cms_ready")
        sum_ready = sem("sum_ready")
        x2_ready = sem("x2_ready")

        def lane_a(layer, c):
            return c if layer == 0 else CHUNKS + c

        def chain_bank(layer, c):
            if layer == 0:
                return 4 + c % 3
            if layer == 2:
                return 4 + c % 2
            return 6 if c < EARLY or c % 2 else 3

        def turn_bank(layer, c):
            return 7 if layer == 0 or c < EARLY or c % 2 else 2

        def ring_bank(phase, j):
            return 2 + j % (3 if phase < 3 else 2)

        def first_final(c):
            return 1 + sum(WB * (c + 1) * S > tok for tok, _ in PHASES[3:])

        def half_of(phase):
            lo, width = PHASES[phase]
            return lo // HALF, slice(lo % HALF, lo % HALF + width)

        def rows(w, t):
            return a[w][t * P:(t + 1) * P, :]

        def four_tiles(w, t):
            return a[w][t * 4 * P:(t + 1) * 4 * P, :].rearrange("(k p) n -> p k n", p=P)

        def wide(slot):
            return stage[slot][:, :]

        def tiled(slot):
            return stage[slot][:, :].rearrange("p (k n) -> p k n", n=D)

        pieces = []
        for t in range(KD):
            pieces.append((rows("L1_cond_cW1", t), wide, [w[:, t, :] for w in cw1]))
        for t in range(2):
            pieces.append((four_tiles("L1_cond_cW2", t), tiled, [w[:, 4 * t:4 * t + 4, :] for w in cw2]))
        for t in range(2 * KD):
            pieces.append((rows("L1_cond_mW1", t), wide, [w[:, t, :] for w in mw1]))
        for t in range(2):
            pieces.append((four_tiles("L1_cond_mW2", t), tiled, [w[:, 4 * t:4 * t + 4, :] for w in mw2]))

        def filling(p):
            return (p + 2) % STAGE, (p + 2) // STAGE + 1

        down_w = {0: "L0_cond_W_down", 2: "L2_cond_W_down", 3: "L3_cond_W_down"}
        up_w = {0: "L0_cond_W_up", 2: "L2_cond_W_up", 3: "L3_cond_W_up"}

        block = ctx.enter_context(nc.Block())

        @block.sync
        def _(sp):
            sp.dma_start(roles_i[:, :], a["itok_B_1_2"].partition_broadcast(P)).then_inc(ids_in, 16)
            sp.dma_start(role_col_i[:, 0:1], a["itok_B_1_2"].rearrange("(b o) -> b o", o=1)).then_inc(ids_in, 16)
            sp.dma_start(role_col_i[:, 1:2], a["itok_B_17_1546"].rearrange("(b o) -> b o", o=1)).then_inc(ids_in, 16)
            for n, pair in enumerate((("L1_cond_Wq", "L1_cond_Wk"), ("L1_cond_Wv", "L1_cond_Wp"))):
                for m, w in enumerate(pair):
                    sp.dma_start(tiled(n)[:, KD * m:KD * (m + 1), :],
                                 a[w].rearrange("(k p) n -> p k n", p=P)).then_inc(stage_in[n], 16)

            def piece(p):
                slot, _ = filling(p)
                src, view, _ = pieces[p]
                if p == 1:
                    sp.wait_ge(wT_ps, 2)
                elif p == 2:
                    sp.wait_ge(fold_ps, KD)
                elif p > 2:
                    sp.wait_ge(w_ready, p - STAGE + 1)
                sp.dma_start(view(slot), src).then_inc(stage_in[slot], 16)

            role = []

            def adapter_weights(layer, c):
                if layer == 3:
                    slot, down, up, done = c % WSLOTS, wdB, wuB, wB_in
                    if c >= WSLOTS:
                        sp.wait_ge(upB_ps, c - WSLOTS + 1)
                else:
                    i = lane_a(layer, c)
                    slot, down, up, done = i % WSLOTS, wdA, wuA, wA_in
                    if i >= WSLOTS:
                        sp.wait_ge(upA_ps, i - WSLOTS + 1)
                r = role[c]
                sp.dma_start(down[slot][:, :, :],
                             a[down_w[layer]].rearrange("r (k p) n -> r p k n", p=P)[bass.ds(r, 1), :, :, :]
                             .rearrange("r p k n -> (r p) k n")).then_inc(done[slot], 16)
                sp.dma_start(up[slot][:, :],
                             a[up_w[layer]][bass.ds(r, 1), :, :].rearrange("r p n -> (r p) n")).then_inc(done[slot], 16)

            sp.wait_ge(chunks_ready, 1)
            for c in range(CHUNKS):
                role.append(sp.value_load(chunk_role_i[0:1, c:c + 1], min_val=0, max_val=R - 1))
                adapter_weights(0, c)
                if c == 0:
                    sp.wait_ge(constants, 1)
                    for n, w in enumerate(("L0_cond_b_up", "L2_cond_b_up", "L3_cond_b_up")):
                        sp.dma_start(bu_rows[32 * n:32 * n + 2 * R, :],
                                     a[w].unsqueeze(0).to_broadcast([2, R, D])).then_inc(bu_in, 16)
                if c in (4, 7):
                    piece((4, 7).index(c))
            for name, w in (("gamma3", "L3_cond_ln_w"), ("beta3", "L3_cond_ln_b")):
                sp.dma_start(table[name][:, :, :], a[w].partition_broadcast(P)).then_inc(tables_in, 16)
            piece(2)
            piece(3)
            for c in range(WSLOTS):
                adapter_weights(2, c)
                adapter_weights(3, c)
            for p in range(4, len(pieces)):
                piece(p)
            for c in range(WSLOTS, CHUNKS):
                adapter_weights(2, c)
                adapter_weights(3, c)

        @block.tensor
        def _(pe):
            read = [None] * 8

            def take(b, done, value):
                if read[b]:
                    pe.wait_ge(*read[b])
                read[b] = (done, value)

            def split_matmul(dst, w, x, first, last):
                pe.matmul(dst, w[0], x[0], start=first, stop=False)
                pe.matmul(dst, w[0], x[1], start=False, stop=False)
                return pe.matmul(dst, w[1], x[0], start=False, stop=last)

            def vectors():
                pe.wait_ge(constants, 1)
                pe.wait_ge(vectors_in, 7 * 16)
                pe.wait_ge(mlp_vectors_in, 5 * 16)
                take(0, vectors_ready, 1)
                pe.transpose(bank[0][:, 0:ROWS], vec_rows[:, :], ident[0:ROWS, 0:ROWS]).then_inc(vectors_ps, 1)

            def find_order():
                pe.wait_ge(sorts_ready, 1)
                pe.wait_ge(spread_ready, 1)
                take(1, order_ready, 1)
                for n in range(2):
                    mm = pe.matmul(bank[1][:, n * POS:(n + 1) * POS], spread[:, n, :], sorts[:, :],
                                   start=True, stop=True)
                mm.then_inc(order_ps, 1)

            def fold_transpose(part):
                pe.wait_ge(constants, 1)
                for n, (slot, half) in ((0, (0, 0)), (1, (0, 1))) if part == 0 else ((2, (1, 0)),):
                    pe.wait_ge(stage_in[slot], 32)
                    take(2 + n, wT_ready, n + 1)
                    for i in range(KD):
                        for t in range(KD):
                            tr = pe.transpose(bank[2 + n][:, t * D + i * P:t * D + (i + 1) * P],
                                              tiled(slot)[:, KD * half + i, t * P:(t + 1) * P], ident[:, :])
                    tr.then_inc(wT_ps, 1)

            def fold(n, m):
                left, right = (("q", "k"), ("v", None))[n]
                if m == 0:
                    take(2 * n + 1, fold_ready, n + 1)
                    pe.wait_ge(wT_ready, 2 + n)
                for t in range(KD):
                    moving = wT[right][:, t, :] if right else tiled(1)[:, KD + t, :]
                    mm = pe.matmul(bank[2 * n + 1][:, m * D:(m + 1) * D], wT[left][:, t, m * P:(m + 1) * P],
                                   moving, start=(t == 0), stop=(t == KD - 1))
                if m == KD - 1:
                    mm.then_inc(fold_ps, 1)

            def load(layer, c):
                if layer:
                    return
                b = chain_bank(0, c)
                take(b, sumA_ready, c + 1)
                pe.wait_ge(x_in[c % TSLOTS], 16 * (c // TSLOTS + 1))
                for m in range(KD):
                    tr = pe.transpose(bank[b][:, m * P:(m + 1) * P], x_tok[c % TSLOTS][:, m * P:(m + 1) * P], ident[:, :])
                tr.then_inc(xT_ps, 1)

            def down(layer, c):
                b = chain_bank(layer, c)
                if layer == 3:
                    take(b, sumB_ready, c + 1)
                    pe.wait_ge(wB_in[c % WSLOTS], 32 * (c // WSLOTS + 1))
                    pe.wait_ge(zB_ready, c + 1)
                    w, x, done = wdB[c % WSLOTS], zB[c % XSLOTS], downB_ps
                else:
                    i = lane_a(layer, c)
                    if layer == 2:
                        take(b, sumA_ready, i + 1)
                    pe.wait_ge(wA_in[i % WSLOTS], 32 * (i // WSLOTS + 1))
                    pe.wait_ge(xA_ready, i + 1)
                    w, x, done = wdA[i % WSLOTS], xA[i % XSLOTS], downA_ps
                if layer:
                    for m in range(KD):
                        pe.transpose(bank[b][:, m * P:(m + 1) * P], x[:, m, :], ident[:, :])
                for k in range(KD):
                    mm = pe.matmul(bank[b][:, D:D + P], w[:, k, :], x[:, k, :], start=(k == 0), stop=(k == KD - 1))
                mm.then_inc(done, 1)

            def up(layer, c):
                dst = bank[chain_bank(layer, c)][:, 0:D]
                if layer == 3:
                    pe.wait_ge(resB_ready, c + 1)
                    h, w, done = hB[c % XSLOTS], wuB[c % WSLOTS], upB_ps
                else:
                    i = lane_a(layer, c)
                    pe.wait_ge(hA_ready if layer == 0 else resA_ready, c + 1)
                    h, w, done = hA[i % XSLOTS], wuA[i % WSLOTS], upA_ps
                if c == 0 and layer == 0:
                    pe.wait_ge(bu_ready, 1)
                    pe.wait_ge(hot_ready, 1)
                lo = 32 * (0, 2, 3).index(layer)
                pe.matmul(dst, hot[lo:lo + 2 * R, c, :], bu[lo:lo + 2 * R, :], start=True, stop=False)
                pe.matmul(dst, h[:, :], w[:, :], start=False, stop=True).then_inc(done, 1)

            def turn(layer, c):
                b, i = turn_bank(layer, c), lane_a(layer, c)
                take(b, *((x1_window, KD * (c + 1)) if layer == 0 else (zB_ready, c + 1)))
                pe.wait_ge(normA_ready, i + 1)
                for m in range(KD):
                    tr = pe.transpose(bank[b][:, m * P:(m + 1) * P], yA[i % YSLOTS][:, m * P:(m + 1) * P], ident[:, :])
                tr.then_inc(normA_T_ps, 1)

            def windows_done(h):
                pe.wait_ge(x1_window, KD * (HALF_WINDOWS if h == 0 else CHUNKS))

            def tokens(h):
                windows_done(h)
                for q in range(2):
                    take(2 + q, tokens_ready, 2 * h + q + 1)
                    for n in range(2):
                        for m in range(KD):
                            lo = h * HALF + (2 * q + n) * P
                            tr = pe.transpose(bank[2 + q][:, n * D + m * P:n * D + (m + 1) * P],
                                              x1T[:, m, lo:lo + P], ident[:, :])
                    tr.then_inc(tokens_ps, 1)

            def pair(base, w, x, done, read_by, h):
                for m in range(KD):
                    take(base + m, read_by, KD * h + m + 1)
                    for k in range(KD):
                        mm = split_matmul(bank[base + m][:, :], [v[:, k, m * P:(m + 1) * P] for v in w],
                                          [v[:, k, :] for v in x], k == 0, k == KD - 1)
                    mm.then_inc(done, 1)

            def project(h):
                pe.wait_ge(fold_ready, 1)
                pe.wait_ge(x1_split, h + 1)
                pair(PROJECT_BANKS[h], wqk, x1, project_ps, y_ready, h)

            def scores(h):
                pe.wait_ge(y_ready, KD * (h + 1))
                take(SCORE_BANKS[h], dots_copied, h + 1)
                for n in range(G):
                    for k in range(KD):
                        mm = pe.matmul(bank[SCORE_BANKS[h]][:, n * P:(n + 1) * P], y_T[:, k, n * P:(n + 1) * P],
                                       x1T[:, k, h * HALF + n * P:h * HALF + (n + 1) * P],
                                       start=(k == 0), stop=(k == KD - 1))
                mm.then_inc(scores_ps, 1)

            def mix(h):
                pe.wait_ge(tokens_ready, 2 * (h + 1))
                pe.wait_ge(probs_ready, h + 1)
                for m in range(KD):
                    take(m, z_ready, KD * h + m + 1)
                    for n in range(G):
                        mm = pe.matmul(bank[m][:, n * P:(n + 1) * P], x1_tok[:, n, m * P:(m + 1) * P],
                                       probs_T[:, n, :], start=True, stop=True)
                    mm.then_inc(mix_ps, 1)

            def attend(h):
                pe.wait_ge(fold_ready, 2)
                pe.wait_ge(z_ready, KD * (h + 1))
                pair(0, wvp, z, attend_ps, ao_ready, h)

            def hidden(phase, j):
                (h, cols), n = half_of(phase), phase * JT + j
                b = ring_bank(phase, j)
                take(b, g_high, n + 1)
                if phase < 2:
                    pe.wait_ge(w_ready, KD)
                    pe.wait_ge(ao_ready, KD * (h + 1))
                    w, x = cw1, [(ao[h], k) for k in range(KD)]
                else:
                    pe.wait_ge(w_ready, 8)
                    pe.wait_ge(cms_ready, KD * (h + 1))
                    w, x = mw1, [(ao[h], k) for k in range(KD)] + [(cms[h], k) for k in range(KD)]
                for k, (v, kk) in enumerate(x):
                    mm = split_matmul(bank[b][:, 0:PHASES[phase][1]], [u[:, k, j * P:(j + 1) * P] for u in w],
                                      [u[:, kk, cols] for u in v], k == 0, k == len(x) - 1)
                mm.then_inc(hidden_ps, 1)

            def outer(phase, part):
                w = cw2 if phase < 2 else mw2
                if part == 0:
                    for m in range(KD):
                        if phase < 2:
                            take(m, cms_full_ready, KD * phase + m + 1)
                        else:
                            take(m, x2_ready, KD * (phase - 2) + m + 1)
                    pe.wait_ge(w_ready, 4 if phase < 2 else 10)
                width = PHASES[phase][1]
                for q in range(JT // 2) if phase < 3 else (part,):
                    tiles = (2 * q, 2 * q + 1)
                    pe.wait_ge(g_ready, phase * JT + tiles[-1] + 1)
                    for m in range(KD):
                        for k in tiles:
                            mm = split_matmul(bank[m][:, 0:width], [v[:, k, m * P:(m + 1) * P] for v in w],
                                              [v[:, k, 0:width] for v in g], k == 0, k == JT - 1)
                        if k == JT - 1:
                            mm.then_inc(outer_ps, 1)

            do = {"vectors": vectors, "order": find_order, "fold_transpose": fold_transpose, "fold": fold,
                  "load": load, "down": down, "up": up, "turn": turn, "tokens": tokens, "project": project, "scores": scores, "mix": mix, "attend": attend,
                  "hidden": hidden, "outer": outer}
            for name, *args in steps:
                if name in do:
                    do[name](*args)

        @block.scalar
        def _(act):
            act.wait_ge(constants, 2)
            act.activation(gelu_first[:, :], part_col[:, :], ACT.Gelu)
            act.wait_ge(ids_in, 48)
            act.copy(spread[:, 0, :], part_col[0:B, :].to_broadcast([B, P]))
            act.copy(spread[:, 1, :], role_col_i[:, 1:2].to_broadcast([B, P])).then_inc(spread_ready, 1)
            for kind, w in enumerate(("L0_cond_b_down", "L2_cond_b_down", "L3_cond_b_down")):
                act.dma_start(vec_rows[R * kind:R * (kind + 1), :], a[w]).then_inc(vectors_in, 16)
            for v, w in ((GAMMA0, "L0_cond_gamma"), (BETA0, "L0_cond_beta"), (GAMMA2, "L2_cond_gamma"),
                         (BETA2, "L2_cond_beta")):
                act.dma_start(vec_rows[R * v:R * (v + KD), :],
                              a[w].rearrange("r (m f) -> (r m) f", f=P)).then_inc(vectors_in, 16)

            first_tok = []

            def load_first_toks(count):
                for c in range(len(first_tok), len(first_tok) + count):
                    first_tok.append(act.value_load(start_tok_i[0:1, c:c + 1], min_val=0, max_val=N))

            def vectors():
                act.wait_ge(chunks_ready, 1)
                load_first_toks(CHUNKS - 2 * XSLOTS)
                act.wait_ge(vectors_ps, 1)
                act.copy(vecs[:, :], bank[0][:, 0:ROWS]).then_inc(vectors_ready, 1)

            def fold_transpose(part):
                for n, w in ((0, "q"), (1, "k")) if part == 0 else ((2, "v"),):
                    act.wait_ge(wT_ps, n + 1)
                    act.copy(wT[w][:, :, :].rearrange("p t n -> p (t n)"), bank[2 + n][:, :]).then_inc(wT_ready, 1)

            def fold(n, m):
                if m < KD - 1:
                    return
                act.wait_ge(fold_ps, n + 1)
                act.copy((wqk, wvp)[n][0][:, :, :].rearrange("p k n -> p (k n)"), bank[2 * n + 1][:, :]).then_inc(fold_high, 1)

            def load(layer, c):
                if layer:
                    return
                act.wait_ge(xT_ps, c + 1)
                if c >= XSLOTS:
                    act.wait_ge(downA_ps, c - XSLOTS + 1)
                act.copy(xA[c % XSLOTS][:, :, :].rearrange("p k n -> p (k n)"),
                         bank[chain_bank(0, c)][:, 0:D]).then_inc(xA_ready, 1)
                if 1 <= c <= XSLOTS:
                    load_first_toks(2)

            def down(layer, c):
                src = bank[chain_bank(layer, c)][:, D:D + P]
                if layer == 3:
                    act.wait_ge(downB_ps, c + 1)
                    if c >= XSLOTS:
                        act.wait_ge(upB_ps, c - XSLOTS + 1)
                    if c >= YSLOTS:
                        act.wait_ge(out_done[c % YSLOTS], 16 * (c // YSLOTS))
                    dst, done = hB[c % XSLOTS], None
                else:
                    i = lane_a(layer, c)
                    act.wait_ge(downA_ps, i + 1)
                    if i >= XSLOTS:
                        act.wait_ge(upA_ps, i - XSLOTS + 1)
                    dst, done = hA[i % XSLOTS], hA_ready if layer == 0 else None
                if layer == 0 and c == 0:
                    act.wait_ge(chunk_vecs_ready, 1)
                ins = act.activation(dst[:, :], src, ACT.Gelu, bias=chunk_vecs[:, BD[(0, 2, 3).index(layer)], c:c + 1])
                if done is not None:
                    ins.then_inc(done, 1)
                if layer:
                    i, y, done = (c, yB, resB_ready) if layer == 3 else (lane_a(2, c), yA, resA_ready)
                    if layer == 2:
                        act.wait_ge(normA_T_ps, i - YSLOTS + 1)
                    act.copy(y[i % YSLOTS][:, :], bank[chain_bank(layer, c)][:, 0:D]).then_inc(done, 1)

            def turn0(c):
                act.wait_ge(normA_T_ps, c + 1)
                if c == 0:
                    act.wait_ge(constants, 3)
                else:
                    act.wait_ge(x1_window, KD * c)
                for m in range(KD):
                    src = bank[turn_bank(0, c)][:, m * P:(m + 1) * P]
                    ins = act.activation(x1T[:, m, bass.ds(first_tok[c], P)], src, ACT.Identity,
                                         bias=chunk_vecs[:, BETA0 + m, c:c + 1],
                                         scale=chunk_vecs[:, GAMMA0 + m, c:c + 1])
                    ins.then_inc(x1_window, 1)

            def turn2(c):
                act.wait_ge(normA_T_ps, lane_a(2, c) + 1)
                if c >= XSLOTS:
                    act.wait_ge(downB_ps, c - XSLOTS + 1)
                for m in range(KD):
                    ins = act.activation(zB[c % XSLOTS][:, m, :], bank[turn_bank(2, c)][:, m * P:(m + 1) * P],
                                         ACT.Identity, bias=chunk_vecs[:, BETA2 + m, c:c + 1],
                                         scale=chunk_vecs[:, GAMMA2 + m, c:c + 1])
                ins.then_inc(zB_ready, 1)

            def tokens(h):
                if h:
                    act.wait_ge(mix_ps, KD * h)
                for q in range(2):
                    act.wait_ge(tokens_ps, 2 * h + q + 1)
                    act.copy(x1_tok[:, 2 * q:2 * q + 2, :].rearrange("p g n -> p (g n)"),
                             bank[2 + q][:, :]).then_inc(tokens_ready, 1)

            def project(h):
                if h:
                    act.wait_ge(scores_ps, h)
                for m in range(KD):
                    act.wait_ge(project_ps, KD * h + m + 1)
                    act.copy(y_T[:, m, :], bank[PROJECT_BANKS[h] + m][:, :]).then_inc(y_ready, 1)

            def scores(h):
                act.wait_ge(dots_ready, h + 1)
                act.activation(weighed[:, :, :].rearrange("p g n -> p (g n)"),
                               dots[:, :, :].rearrange("p g n -> p (g n)"), ACT.Exp, scale=SCALE).then_inc(exp_ready, 1)

            def mix(h):
                if h:
                    act.wait_ge(attend_ps, KD * h)
                for m in range(KD):
                    act.wait_ge(mix_ps, KD * h + m + 1)
                    act.copy(z[0][:, m, :], bank[m][:, :]).then_inc(z_high, 1)

            def attend(h):
                for m in range(KD):
                    act.wait_ge(attend_ps, KD * h + m + 1)
                    act.activation(ao[h][0][:, m, :], bank[m][:, :], ACT.Identity,
                                   bias=vecs[:, BP + m:BP + m + 1]).then_inc(ao_high, 1)

            def hidden(phase, j):
                n, width = phase * JT + j, PHASES[phase][1]
                b = ring_bank(phase, j)
                act.wait_ge(hidden_ps, n + 1)
                bias = vecs[:, (CB1 if phase < 2 else MB1) + j:(CB1 if phase < 2 else MB1) + j + 1]
                if n >= 2:
                    act.wait_ge(g_ready, n - 1)
                act.activation(g_full[n % 2][:, 0:width], bank[b][:, 0:width], ACT.Gelu, bias=bias)
                if phase and j == 0:
                    act.wait_ge(outer_ps, KD * phase)
                act.activation(g[0][:, j, 0:width], bank[b][:, 0:width], ACT.Gelu,
                               bias=bias).then_inc(g_high, 1)

            def outer(phase, part):
                if phase < 2:
                    if phase:
                        act.wait_ge(outer_ps, 2 * KD)
                    for m in range(KD):
                        act.wait_ge(cms_full_ready, KD * phase + m + 1)
                        act.copy(cms[phase][0][:, m, :], cms_full[:, m, :]).then_inc(cms_high, 1)

            do = {"vectors": vectors, "fold_transpose": fold_transpose, "fold": fold,
                  "load": load, "down": down, "turn": lambda layer, c: (turn2 if layer else turn0)(c), "tokens": tokens,
                  "project": project, "scores": scores, "mix": mix, "attend": attend,
                  "hidden": hidden, "outer": outer}
            for name, *args in steps:
                if name in do:
                    do[name](*args)

        @block.vector
        def _(dve):
            own = [0]

            def link(ins):
                own[0] += 1
                ins.then_inc(dve_own, 1)
                dve.wait_ge(dve_own, own[0])

            def then(ins):
                own[0] += 1
                ins.then_inc(dve_own, 1)
                dve.wait_ge(dve_own, own[0] - 1)

            def find_windows():
                dve.wait_ge(constants, 2)
                link(dve.tensor_scalar(past[:, :], seq_from[:, :], part_col[:, 0:1], None, ALU.is_le))
                link(dve.tensor_reduce(seq_col[:, :], past[:, :], X_AXIS, ALU.add))
                link(dve.scalar_tensor_tensor(out=tok_col[:, :], in0=seq_col[:, :], scalar=-float(S),
                                              in1=part_col[:, :], op0=ALU.mult, op1=ALU.add))
                dve.tensor_scalar(tok_spare[:, :], seq_col[:, :], -float(S), -float(N), ALU.mult, ALU.add)
                link(dve.tensor_scalar(low_row[:, :], tok_col[:, :], float(R), -1.0, ALU.is_ge, ALU.mult))
                dve.scalar_tensor_tensor(out=role_row_of[:, :], in0=low_row[:, :], scalar=float(R),
                                         in1=tok_col[:, :], op0=ALU.mult, op1=ALU.add)
                dve.wait_ge(ids_in, 48)
                then(dve.tensor_scalar(roles[:, :], roles_i[:, :], 0.0, float(R - 1), ALU.max, ALU.min))
                then(dve.tensor_scalar(key_col[:, 0:1], role_col_i[:, 0:1], 0.0, float(R - 1), ALU.max, ALU.min))
                then(dve.tensor_tensor(is_role[:, :, :], roles[:, :].unsqueeze(1).to_broadcast([P, R, B]),
                                       role_row[:, :, :], ALU.is_equal))
                then(dve.tensor_scalar(key_col[:, 0:1], key_col[:, 0:1], float(B), part_col[0:B, :], ALU.mult, ALU.add))
                then(dve.tensor_reduce(count[:, :], is_role[:, :, :], X_AXIS, ALU.add))
                then(dve.scalar_tensor_tensor(out=keys[:, :], in0=roles[:, :], scalar=float(B),
                                              in1=pos_row[:, 0:B], op0=ALU.mult, op1=ALU.add))
                then(dve.tensor_tensor(more[:, :, :], count[:, :].unsqueeze(2).to_broadcast([P, R, 8]),
                                       four_row[:, :, :], ALU.is_gt))
                then(dve.tensor_scalar(below[:, :], keys[0:B, :], key_col[:, 0:1], None, ALU.is_lt))
                then(dve.tensor_reduce(wins[:, :], more[:, :, :], X_AXIS, ALU.add))
                then(dve.tensor_reduce(pos_col[:, :], below[:, :], X_AXIS, ALU.add))
                dve.tensor_scalar(ends4[:, 0:1], wins[:, 0:1], float(WB), None, ALU.mult)
                then(dve.tensor_scalar(ends4[:, 1:2], wins[:, 1:2], wins[:, 0:1], float(WB), ALU.add, ALU.mult))
                dve.tensor_scalar(sorts[:, :], pos_row[0:B, :], pos_col[:, 0:1], None,
                                  ALU.is_equal).then_inc(sorts_ready, 1)
                link(dve.scalar_tensor_tensor(out=short[:, :], in0=wins[:, 0:2], scalar=-float(WB),
                                              in1=count[:, 0:2], op0=ALU.mult, op1=ALU.add))
                link(dve.tensor_tensor(later[:, :, :], chunk4_row[:, :].unsqueeze(1).to_broadcast([P, 2, CHUNKS]),
                                       ends4[:, :].unsqueeze(2).to_broadcast([P, 2, CHUNKS]), ALU.is_ge))
                dve.tensor_tensor(chunk_role[:, :], later[:, 0, :], later[:, 1, :], ALU.add)
                link(dve.scalar_tensor_tensor(out=start[:, :], in0=later[:, 0, :], scalar=short[:, 0:1],
                                              in1=chunk4_row[:, :], op0=ALU.mult, op1=ALU.add))
                link(dve.scalar_tensor_tensor(out=start[:, :], in0=later[:, 1, :], scalar=short[:, 1:2],
                                              in1=start[:, :], op0=ALU.mult, op1=ALU.add))
                link(dve.tensor_tensor(reach[:, :, :], pos_row[:, :].unsqueeze(1).to_broadcast([P, CHUNKS, POS]),
                                       start[:, :].unsqueeze(2).to_broadcast([P, CHUNKS, POS]), ALU.subtract))
                dve.tensor_copy(chunk_role_i[:, :], chunk_role[:, :])
                dve.tensor_scalar(start_tok_i[:, :], start[:, :], float(B), float(S), ALU.min,
                                  ALU.mult).then_inc(chunks_ready, 1)

            def find_order():
                dve.wait_ge(order_ps, 1)
                link(dve.scalar_tensor_tensor(out=reach[:, :, :], in0=reach[:, :, :], scalar=seq_col[:, 0:1],
                                              in1=bank[1][:, 0:POS].unsqueeze(1).to_broadcast([P, CHUNKS, POS]),
                                              op0=ALU.is_equal, op1=ALU.mult))
                link(dve.tensor_reduce(seq_at[:, :], reach[:, :, :], X_AXIS, ALU.add))
                dve.tensor_scalar(from_row_i[:, :], seq_at[:, :], float(S), tok_col[:, 0:1],
                                  ALU.mult, ALU.add).then_inc(rows_in_ready, 1)
                dve.tensor_scalar(hot_col[:, :], chunk_role[:, :], role_row_of[:, 0:1], None, ALU.is_equal)
                dve.tensor_copy(codes[:, :], bank[1][:, POS:2 * POS]).then_inc(order_ready, 1)
                link(dve.tensor_scalar(end[:, :], later[:, 0, :], count[:, 1:2], count[:, 0:1], ALU.mult, ALU.add))
                link(dve.scalar_tensor_tensor(out=end[:, :], in0=later[:, 1, :], scalar=count[:, 2:3],
                                              in1=end[:, :], op0=ALU.mult, op1=ALU.add))
                dve.scalar_tensor_tensor(out=valid[:, :], in0=start[:, :], scalar=seq_col[:, 0:1], in1=end[:, :],
                                         op0=ALU.add, op1=ALU.is_lt)
                link(dve.tensor_scalar(row_at[:, :], seq_at[:, :], float(S), tok_spare[:, 0:1], ALU.mult, ALU.add))
                link(dve.tensor_tensor(row_at[:, :], row_at[:, :], valid[:, :], ALU.mult))
                dve.tensor_scalar(row_at_i[:, :], row_at[:, :], spare_col[:, 0:1], None, ALU.add).then_inc(rows_ready, 1)
                dve.tensor_copy(hot[:, :, :], hot_col[:, :].unsqueeze(2).to_broadcast([P, CHUNKS, P])).then_inc(hot_ready, 1)

            def vectors():
                dve.wait_ge(vectors_ready, 1)
                link(dve.tensor_tensor(role_hot[:, :, :], chunk_role[:, :].unsqueeze(2).to_broadcast([P, CHUNKS, R]),
                                       role_in[:, :, :], ALU.is_equal))
                for v in range(PER_ROLE):
                    mine = (vecs[:, R * v:R * (v + 1)] if v in BD else
                            vecs[:, R * GAMMA0:BP].rearrange("p (v r m) -> p v m r", r=R, m=KD)
                            [:, (v - GAMMA0) // KD, (v - GAMMA0) % KD, :])
                    ins = dve.tensor_tensor(picked[:, v, :, :], role_hot[:, :, :],
                                            mine.unsqueeze(1).to_broadcast([P, CHUNKS, R]), ALU.mult)
                link(ins)
                dve.tensor_reduce(chunk_vecs[:, :, :], picked[:, :, :, :], X_AXIS, ALU.add).then_inc(chunk_vecs_ready, 1)
                dve.wait_ge(bu_in, 3 * 16)
                dve.tensor_copy(bu_high[:, :], bu_rows[:, :]).then_inc(bu_high_ready, 1)
                dve.wait_ge(bu_high_ready, 1)
                dve.scalar_tensor_tensor(out=bu[:, :], in0=bu_high[:, :].bitcast(F32), scalar=low_row[:, 0:1],
                                         in1=bu_rows[:, :], op0=ALU.mult, op1=ALU.add).then_inc(bu_ready, 1)
                for m in range(KD):
                    ins = dve.tensor_scalar(target[:, m, :], codes[:, :], (part_col, part_col2)[m][:, 0:1],
                                            vecs[:, CB2 + m:CB2 + m + 1], ALU.is_equal, ALU.add)
                ins.then_inc(target_ready, 1)

            def fold(n):
                dve.wait_ge(fold_high, n + 1)
                w = (wqk, wvp)[n]
                dve.tensor_tensor(w[1][:, :, :].rearrange("p k n -> p (k n)"), bank[2 * n + 1][:, :],
                                  w[0][:, :, :].rearrange("p k n -> p (k n)").bitcast(F32),
                                  ALU.subtract).then_inc(fold_ready, 1)

            def weights(p):
                slot, fill = filling(p)
                _, view, parts = pieces[p]
                if p == 4:
                    dve.wait_ge(attend_ps, 2 * KD)
                if p == 8:
                    dve.wait_ge(hidden_ps, 2 * JT)
                dve.wait_ge(stage_in[slot], 16 * fill + (16 if slot < 2 else 0))
                dve.tensor_copy(parts[0], view(slot)).then_inc(w_high, 1)

            def moments(y, x, st, mv, k, bank_ap, done, summed, n):
                dve.tensor_tensor(y, bank_ap, x, ALU.add).then_inc(summed, 1)
                dve.wait_ge(summed, n + 1)
                link(dve.bn_stats(st[:, k, :], y))
                dve.bn_aggr(mv[:, k, :], st[:, k, :]).then_inc(done, 1)

            first_tok, role = [], []

            def load(layer, c):
                if layer == 0:
                    return
                i = lane_a(2, c)
                dve.wait_ge(x2_ready, KD * first_final(c))
                dve.wait_ge(downA_ps, i - XSLOTS + 1)
                dve.tensor_scalar(xA[i % XSLOTS][:, :, :], x1T[:, :, bass.ds(first_tok[c], P)], 0.0, 1.0,
                                  ALU.max, ALU.min).then_inc(xA_ready, 1)

            def up(layer, c):
                if layer == 3:
                    k = c % YSLOTS
                    y = yB[k][:, :]
                    dve.wait_ge(upB_ps, c + 1)
                    moments(y, y, statsB, mvB, k, bank[chain_bank(3, c)][:, 0:D], varB_ready, sumB_ready, c)
                else:
                    i = lane_a(layer, c)
                    k = i % YSLOTS
                    y = yA[k][:, :]
                    if layer == 0 and c >= YSLOTS:
                        dve.wait_ge(normA_T_ps, c - YSLOTS + 1)
                    dve.wait_ge(upA_ps, i + 1)
                    moments(y, x_tok[c % TSLOTS][:, :] if layer == 0 else y, statsA, mvA, k,
                            bank[chain_bank(layer, c)][:, 0:D], varA_ready, sumA_ready, i)

            def center(layer, c):
                i = lane_a(layer, c)
                k = i % YSLOTS
                dve.wait_ge(rstdA_ready, i + 1)
                dve.tensor_scalar(yA[k][:, :], yA[k][:, :], mvA[:, k, 0:1], rstdA[:, k, 1:2],
                                  ALU.subtract, ALU.mult).then_inc(normA_ready, 1)

            def finish(layer, c):
                k = c % YSLOTS
                r = role[c]
                if c == 0:
                    dve.wait_ge(tables_in, 2 * 16)
                dve.wait_ge(rstdB_ready, c + 1)
                link(dve.scalar_tensor_tensor(out=yB[k][:, :], in0=yB[k][:, :], scalar=mvB[:, k, 0:1],
                                              in1=table["gamma3"][:, bass.ds(r, 1), :].rearrange("p r n -> p (r n)"),
                                              op0=ALU.subtract, op1=ALU.mult))
                dve.scalar_tensor_tensor(out=yB[k][:, :], in0=yB[k][:, :], scalar=rstdB[:, k, 1:2],
                                         in1=table["beta3"][:, bass.ds(r, 1), :].rearrange("p r n -> p (r n)"),
                                         op0=ALU.mult, op1=ALU.add).then_inc(out_ready, 1)

            def split(h):
                dve.wait_ge(x1_window, KD * (HALF_WINDOWS if h == 0 else CHUNKS))
                if h:
                    dve.wait_ge(project_ps, KD * h)
                src = x1T[:, :, h * HALF:(h + 1) * HALF]
                link(dve.tensor_copy(x1[0][:, :, :], src))
                dve.tensor_tensor(x1[1][:, :, :], src, x1[0][:, :, :].bitcast(F32), ALU.subtract).then_inc(x1_split, 1)

            def scores(h):
                dve.wait_ge(scores_ps, h + 1)
                for q in range(WB):
                    lo, hi = S * q, S * (q + 1)
                    src = bank[SCORE_BANKS[h]][lo:hi, :].rearrange("p (g n) -> p g n", n=P)
                    ins = dve.tensor_copy(dots[lo:hi, :, :], src[:, :, lo:hi])
                ins.then_inc(dots_copied, 1)
                dve.wait_ge(dots_copied, h + 1)
                link(dve.tensor_reduce(peak[:, :], dots[:, :, :], X_AXIS, ALU.max))
                dve.tensor_tensor(dots[:, :, :], dots[:, :, :], peak[:, :].unsqueeze(2).to_broadcast([P, G, S]),
                                  ALU.subtract).then_inc(dots_ready, 1)

            def soften(h):
                dve.wait_ge(exp_ready, h + 1)
                link(dve.tensor_reduce(total[:, :], weighed[:, :, :], X_AXIS, ALU.add))
                link(dve.reciprocal(inv_total[:, :], total[:, :]))
                link(dve.tensor_tensor(probs[:, :, :], weighed[:, :, :],
                                       inv_total[:, :].unsqueeze(2).to_broadcast([P, G, S]), ALU.mult))
                if h:
                    dve.wait_ge(mix_ps, KD * h)
                else:
                    dve.wait_ge(constants, 3)
                for q in range(WB):
                    lo, hi = S * q, S * (q + 1)
                    ins = dve.transpose(probs_T[lo:hi, :, lo:hi], probs[lo:hi, :, :])
                ins.then_inc(probs_ready, 1)

            def mix(h):
                for m in range(KD):
                    dve.wait_ge(z_high, KD * h + m + 1)
                    dve.tensor_tensor(z[1][:, m, :], bank[m][:, :], z[0][:, m, :].bitcast(F32),
                                      ALU.subtract).then_inc(z_ready, 1)

            def attend(h):
                for m in range(KD):
                    dve.wait_ge(ao_high, KD * h + m + 1)
                    dve.scalar_tensor_tensor(out=ao[h][1][:, m, :], in0=bank[m][:, :],
                                             scalar=vecs[:, BP + m:BP + m + 1], in1=ao[h][0][:, m, :].bitcast(F32),
                                             op0=ALU.add, op1=ALU.subtract).then_inc(ao_ready, 1)

            def hidden(phase, j):
                n, width = phase * JT + j, PHASES[phase][1]
                dve.wait_ge(g_high, n + 1)
                dve.tensor_tensor(g[1][:, j, 0:width], g_full[n % 2][:, 0:width], g[0][:, j, 0:width].bitcast(F32),
                                  ALU.subtract).then_inc(g_ready, 1)
                if n < CHUNKS:
                    first_tok.append(dve.value_load(start_tok_i[0:1, n:n + 1], min_val=0, max_val=N))
                elif n < 2 * CHUNKS:
                    role.append(dve.value_load(chunk_role_i[0:1, n - CHUNKS:n - CHUNKS + 1], min_val=0, max_val=R - 1))

            def outer(phase, part):
                if phase > 2 and part < 3:
                    return
                h = phase % 2
                if phase < 2:
                    if phase == 0:
                        dve.wait_ge(target_ready, 1)
                    else:
                        dve.wait_ge(sum_ready, KD)
                    for m in range(KD):
                        dve.wait_ge(outer_ps, KD * phase + m + 1)
                        dve.tensor_tensor(cms_full[:, m, :].rearrange("p (b s) -> p b s", s=S),
                                          bank[m][:, :].rearrange("p (b s) -> p b s", s=S),
                                          target[:, m, h * (B // 2):(h + 1) * (B // 2)].unsqueeze(2).to_broadcast([P, B // 2, S]),
                                          ALU.add).then_inc(cms_full_ready, 1)
                    for m in range(KD):
                        dve.wait_ge(cms_high, KD * phase + m + 1)
                        dve.tensor_tensor(cms[h][1][:, m, :], cms_full[:, m, :], cms[h][0][:, m, :].bitcast(F32),
                                          ALU.subtract).then_inc(cms_ready, 1)
                else:
                    lo, width = PHASES[phase]
                    dve.wait_ge(sum_ready, KD * (lo // HALF + 1))
                    for m in range(KD):
                        dve.wait_ge(outer_ps, KD * phase + m + 1)
                        part = x1T[:, m, lo:lo + width]
                        dve.scalar_tensor_tensor(out=part, in0=bank[m][:, 0:width],
                                                 scalar=vecs[:, MB2 + m:MB2 + m + 1], in1=part,
                                                 op0=ALU.add, op1=ALU.add).then_inc(x2_ready, 1)

            find_windows()
            do = {"vectors": lambda: None, "order": lambda: (find_order(), vectors()), "fold_low": fold,
                  "weights": weights, "load": load, "up": up, "center": center, "finish": finish,
                  "split": split, "scores": scores, "probs": soften, "mix": mix, "attend": attend,
                  "hidden": hidden, "outer": outer}
            for name, *args in steps:
                if name in do:
                    do[name](*args)

        @block.gpsimd
        def _(pool):
            own = [0]

            def link(ins):
                own[0] += 1
                ins.then_inc(pool_own, 1)
                pool.wait_ge(pool_own, own[0])

            link(pool.memset(ident[:, :], 0.0))
            link(pool.memset(bu_rows[:, :], 0.0))
            pool.affine_select(out=ident[:, :], in_=ident[:, :], compare_op=ALU.not_equal, fill=1.0, base=0,
                               pattern=[[-1, P]], channel_multiplier=1).then_inc(constants, 1)

            def iota(dst, pattern, base=0, mult=0):
                return pool.iota(dst, pattern, base=base, channel_multiplier=mult,
                                 allow_small_or_imprecise_dtypes=True)

            iota(pos_row[:, :], [[1, POS]])
            iota(part_col[:, :], [[0, 1]], 0, 1)
            iota(role_row[:, :, :], [[1, R], [0, B]])
            iota(four_row[:, :, :], [[0, R], [WB, 8]])
            iota(chunk4_row[:, :], [[WB, CHUNKS]])
            iota(role_in[:, :, :], [[0, CHUNKS], [1, R]])
            iota(part_col2[:, :], [[0, 1]], P, 1)
            iota(spare_col[:, :], [[0, 1]], N, 1)
            pool.memset(power[:, :], -0.5)
            iota(seq_from[:, :], [[S, WB - 1]], S, 0).then_inc(constants, 1)
            for row, w, n in ((BP, "L1_cond_bp", KD), (CB1, "L1_cond_cb1", JT), (CB2, "L1_cond_cb2", KD),
                              (MB1, "L1_cond_mb1", JT), (MB2, "L1_cond_mb2", KD)):
                pool.dma_start(vec_rows[row:row + n, :], a[w].rearrange("(n p) -> n p", p=P)).then_inc(mlp_vectors_in, 16)
            pool.memset(x1T[:, :, N:POS * S], 0.0)
            pool.memset(probs_T[:, :, :], 0.0).then_inc(constants, 1)

            def weights(p):
                slot, _ = filling(p)
                _, view, parts = pieces[p]
                pool.wait_ge(w_high, p + 1)
                pool.tensor_tensor(parts[1], view(slot), parts[0].bitcast(F32), ALU.subtract).then_inc(w_ready, 1)

            def gather(c):
                if c >= TSLOTS:
                    pool.wait_ge(sumA_ready, c - TSLOTS + 1)
                pool.indirect_dma_start(
                    out=x_tok[c % TSLOTS][:, :], out_offset=None, in_=a["x"].rearrange("b s d -> (b s) d"),
                    in_offset=bass.IndirectOffsetOnAxis(ap=from_row_i[:, c:c + 1], axis=0)
                    ).then_inc(x_in[c % TSLOTS], 16)

            def find_order():
                pool.wait_ge(rows_in_ready, 1)
                for c in range(TSLOTS):
                    gather(c)

            def rstd(var, mv, k, ready, n, done):
                pool.wait_ge(ready, n)
                link(pool.tensor_scalar(var[:, k, 0:1], mv[:, k, 1:2], LN_EPS, None, ALU.add))
                pool.tensor_tensor(var[:, k, 1:2], var[:, k, 0:1], power[:, :], ALU.pow).then_inc(done, 1)

            def up(layer, c):
                if layer == 3:
                    rstd(rstdB, mvB, c % YSLOTS, varB_ready, c + 1, rstdB_ready)
                else:
                    i = lane_a(layer, c)
                    rstd(rstdA, mvA, i % YSLOTS, varA_ready, i + 1, rstdA_ready)
                if layer == 0 and c + TSLOTS < CHUNKS:
                    gather(c + TSLOTS)

            def finish(layer, c):
                if c == 0:
                    pool.wait_ge(rows_ready, 1)
                pool.wait_ge(out_ready, c + 1)
                pool.indirect_dma_start(
                    out=out.rearrange("b s d -> (b s) d"),
                    out_offset=bass.IndirectOffsetOnAxis(ap=row_at_i[:, c:c + 1], axis=0),
                    in_=yB[c % YSLOTS][:, :], in_offset=None,
                    bounds_check=N - 1, oob_is_err=False).then_inc(out_done[c % YSLOTS], 16)

            def outer(phase, part):
                if phase < 2:
                    for m in range(KD):
                        pool.wait_ge(cms_full_ready, KD * phase + m + 1)
                        half = x1T[:, m, phase * HALF:(phase + 1) * HALF]
                        pool.tensor_tensor(half, half, cms_full[:, m, :], ALU.add).then_inc(sum_ready, 1)

            do = {"order": find_order, "weights": weights, "up": up, "finish": finish, "outer": outer}
            for name, *args in steps:
                if name in do:
                    do[name](*args)
            for k in range(YSLOTS):
                pool.wait_ge(out_done[k], 16 * len(range(k, CHUNKS, YSLOTS)))


def kernel(**inputs):
    import numpy as np
    import concourse.bacc as bacc
    from concourse.bass_utils import run_bass_kernel_spmd

    nc = bacc.Bacc("TRN2", target_bir_lowering=False, num_devices=1)
    arrays, aps = {}, {}
    for name, value in inputs.items():
        if name == "_lenS":
            continue
        v = np.ascontiguousarray(value)
        arrays[f"in_{name}"] = v
        aps[name] = nc.dram_tensor(f"in_{name}", v.shape, mybir.dt.from_np(v.dtype), kind="ExternalInput").ap()
    out = nc.dram_tensor("out", (B, S, D), F32, kind="ExternalOutput").ap()
    build(nc, aps, out)
    return run_bass_kernel_spmd(nc, [arrays], core_ids=[0]).results[0]["out"]
```
